# Optimizing a Trainium2 kernel written in Bass

```python
import numpy as np
import jax
import jax.numpy as jnp

def _softmax(x, axis=-1):
    return jax.nn.softmax(x, axis=axis)

def _gelu(x):
    return jax.nn.gelu(x, approximate=True)

def _silu(x):
    return jax.nn.silu(x)

def _sigmoid(x):
    return jax.nn.sigmoid(x)

def _layernorm(x, axis=-1, eps=1e-05):
    m = jnp.mean(x, axis=axis, keepdims=True)
    v = jnp.var(x, axis=axis, keepdims=True)
    return (x - m) / jnp.sqrt(v + eps)

def _scatter_add(tgt, idx, src, axis=0):
    return tgt.at[idx].add(src)

def _segment_sum(src, seg, n):
    return jax.ops.segment_sum(src, seg, n)
kernel_name = 'mk_metaformer_d1_conv_nchw2048_r4_f9501d'

def setup_inputs(seed: int=0):
    np.random.seed(seed)
    _w = jnp.asarray

    def _rec_inputs():
        import jax
        import jax.numpy as jnp
        _gk = jax.random.key(seed)
        x = -0.0003929 + 0.9999 * jax.random.normal(jax.random.fold_in(_gk, 1), (4, 512, 16, 32), jnp.float32)
        return x
    x = _rec_inputs()

    def _L0_conv_setup():
        import jax, jax.numpy as jnp
        import numpy as np
        B, L, H, D = (4, 512, 16, 32)
        KERNEL_SIZES = (3, 7, 15)
        C = H * D

        def _causal_dwconv(x_flat, w):
            k = w.shape[-1]
            return jax.lax.conv_general_dilated(x_flat, w, window_strides=(1,), padding=[(k - 1, 0)], dimension_numbers=('NCH', 'OIH', 'NCH'), feature_group_count=x_flat.shape[1])
        key = jax.random.key(seed)
        k0, k1, k2, k3, k4 = jax.random.split(key, 5)
        x = jax.random.normal(k0, (B, L, H, D), dtype=jnp.float32)
        w3 = jax.random.normal(k1, (C, 1, 3), dtype=jnp.float32) * 0.02
        w7 = jax.random.normal(k2, (C, 1, 7), dtype=jnp.float32) * 0.02
        w15 = jax.random.normal(k3, (C, 1, 15), dtype=jnp.float32) * 0.02
        bound = 1.0 / np.sqrt(3 * D)
        w_mix = jax.random.uniform(k4, (D, 3 * D), dtype=jnp.float32, minval=-bound, maxval=bound)
        return {'x': x, 'w3': w3, 'w7': w7, 'w15': w15, 'w_mix': w_mix}
    _L0_conv_all = _L0_conv_setup()
    _L0_conv_in = {k: v for k, v in _L0_conv_all.items() if k in ('w3', 'w7', 'w15', 'w_mix')}
    del _L0_conv_all

    def _L0_ffn_setup():
        import jax, jax.numpy as jnp
        import numpy as np
        NUM_EXPERTS = 8
        TOP_K = 2
        FFN_DIM = 512
        HIDDEN_DIM = 1024
        key = jax.random.key(seed)
        k0, k1, k2, k3, k4 = jax.random.split(key, 5)
        scale = 0.02
        return {'hidden_states': jax.random.normal(k0, (2, 256, FFN_DIM), dtype=jnp.float32), 'gate_w': jax.random.normal(k1, (NUM_EXPERTS, FFN_DIM), dtype=jnp.float32) * scale, 'w1': jax.random.normal(k2, (NUM_EXPERTS, FFN_DIM, HIDDEN_DIM), dtype=jnp.float32) * scale, 'w2': jax.random.normal(k3, (NUM_EXPERTS, HIDDEN_DIM, FFN_DIM), dtype=jnp.float32) * scale, 'w3': jax.random.normal(k4, (NUM_EXPERTS, FFN_DIM, HIDDEN_DIM), dtype=jnp.float32) * scale}
    _L0_ffn_all = _L0_ffn_setup()
    _L0_ffn_in = {k: v for k, v in _L0_ffn_all.items() if k in ('gate_w', 'w1', 'w2', 'w3')}
    del _L0_ffn_all
    return {'x': x, 'L0_conv_w3': _L0_conv_in['w3'], 'L0_conv_w7': _L0_conv_in['w7'], 'L0_conv_w15': _L0_conv_in['w15'], 'L0_conv_w_mix': _L0_conv_in['w_mix'], 'L0_ffn_gate_w': _L0_ffn_in['gate_w'], 'L0_ffn_w1': _L0_ffn_in['w1'], 'L0_ffn_w2': _L0_ffn_in['w2'], 'L0_ffn_w3': _L0_ffn_in['w3']}

def reference(x, L0_conv_w3, L0_conv_w7, L0_conv_w15, L0_conv_w_mix, L0_ffn_gate_w, L0_ffn_w1, L0_ffn_w2, L0_ffn_w3):
    import jax
    import jax.numpy as jnp

    def _L0_conv_ref(x, w3, w7, w15, w_mix):
        import jax, jax.numpy as jnp
        import numpy as np
        B, L, H, D = (4, 512, 16, 32)
        KERNEL_SIZES = (3, 7, 15)
        C = H * D

        def _causal_dwconv(x_flat, w):
            k = w.shape[-1]
            return jax.lax.conv_general_dilated(x_flat, w, window_strides=(1,), padding=[(k - 1, 0)], dimension_numbers=('NCH', 'OIH', 'NCH'), feature_group_count=x_flat.shape[1])
        b, l, h, d = x.shape
        n_scales = 3
        x_flat = x.reshape(b, l, h * d).transpose(0, 2, 1)
        outs = [_causal_dwconv(x_flat, w) for w in (w3, w7, w15)]
        y = jnp.concatenate(outs, axis=1)
        y = y.reshape(b, h, n_scales * d, l).transpose(0, 3, 1, 2)
        return jnp.einsum('blhm,dm->blhd', y, w_mix)

    def _L0_ffn_ref(hidden_states, gate_w, w1, w2, w3):
        import jax, jax.numpy as jnp
        import numpy as np
        NUM_EXPERTS = 8
        TOP_K = 2
        FFN_DIM = 512
        HIDDEN_DIM = 1024
        origin_shape = hidden_states.shape
        x = hidden_states.reshape(-1, FFN_DIM)
        n_tokens = x.shape[0]
        router_logits = x @ gate_w.T
        routing_probs = jax.nn.softmax(router_logits.astype(jnp.float32), axis=-1)
        topk_w, topk_idx = jax.lax.top_k(routing_probs, TOP_K)
        topk_w = topk_w / jnp.sum(topk_w, axis=-1, keepdims=True)
        topk_w = topk_w.astype(x.dtype)
        token_ids = jnp.arange(n_tokens)[:, None]
        full_w = jnp.zeros((n_tokens, NUM_EXPERTS), dtype=x.dtype)
        full_w = full_w.at[token_ids, topk_idx].add(topk_w)
        h = jax.nn.silu(jnp.einsum('nf,efh->enh', x, w1)) * jnp.einsum('nf,efh->enh', x, w3)
        y = jnp.einsum('enh,ehf->enf', h, w2)
        out = jnp.einsum('enf,ne->nf', y, full_w)
        return out.reshape(origin_shape)

    def _gn(v, G=32, eps=1e-05):
        B_, C_, H_, W_ = v.shape
        g = v.reshape(B_, G, C_ // G, H_, W_)
        m = jnp.mean(g, axis=(2, 3, 4), keepdims=True)
        s = jnp.var(g, axis=(2, 3, 4), keepdims=True)
        return ((g - m) / jnp.sqrt(s + eps)).reshape(v.shape)

    def _ln_c(v, eps=1e-06):
        m = jnp.mean(v, axis=1, keepdims=True)
        s = jnp.var(v, axis=1, keepdims=True)
        return (v - m) / jnp.sqrt(s + eps)

    def _ln_t(v, eps=1e-05):
        m = jnp.mean(v, axis=-1, keepdims=True)
        s = jnp.var(v, axis=-1, keepdims=True)
        return (v - m) / jnp.sqrt(s + eps)

    def _to_tokens(v):
        B_, C_, H_, W_ = v.shape
        return v.reshape(B_, C_, H_ * W_).transpose(0, 2, 1)

    def _from_tokens(t, like):
        B_, C_, H_, W_ = like.shape
        return t.transpose(0, 2, 1).reshape(B_, C_, H_, W_)
    x = x + _L0_conv_ref(_ln_c(x), L0_conv_w3, L0_conv_w7, L0_conv_w15, L0_conv_w_mix)
    t = _to_tokens(x)
    t = t + _L0_ffn_ref(_ln_t(t), L0_ffn_gate_w, L0_ffn_w1, L0_ffn_w2, L0_ffn_w3)
    x = _from_tokens(t, x)
    return x

_drawn_inputs = setup_inputs


def setup_inputs(seed=0):
    import zlib

    import numpy as np

    out = dict(_drawn_inputs(seed))
    spreads = {}
    factors = {'L0_conv_w3': 4.47, 'L0_conv_w7': 3.127}
    for name, (base, spread) in spreads.items():
        noise = np.random.default_rng([zlib.crc32(name.encode()), seed]).standard_normal(out[name].shape)
        drawn = base * np.exp(spread * noise) if base else spread * noise
        out[name] = jnp.asarray(drawn.astype(out[name].dtype))
    for name, factor in factors.items():
        out[name] = (out[name] * factor).astype(out[name].dtype)
    return out
```

```python
from contextlib import ExitStack

import concourse.bass as bass
from concourse import mybir

F32 = mybir.dt.float32
F32R = mybir.dt.float32r
I32 = mybir.dt.int32
ALU = mybir.AluOpType
ACT = mybir.ActivationFunctionType
AX_X = mybir.AxisListType.X

P = 128
NB = 4
L = 512
C = 512
NQ = L // P
D = 32
NBLK = C // D
TAPS = (3, 7, 15)
NS = len(TAPS)
LAGS = tuple(NQ * -(-(k + NQ - 1) // NQ) for k in TAPS)
PAD = max(LAGS) // NQ - 1
NG = C // P
NT = NB * NG
E = 8
HID = 1024
TILES = NT * 2 + E - 1
SLOT_TILES = TILES + 1
UNITS = 6
RING = 9
EPS_C = 1e-6
EPS_T = 1e-5


def metaformer(nc, x, w3c, w7c, w15c, w_mix, gate_w, w1, w2, w3, out):
    taps_dram = (w3c, w7c, w15c)
    x_nat = x.rearrange("b (i q) h w -> b i q (h w)", q=NQ)
    out_nat = out.rearrange("b (i q) h w -> b i q (h w)", q=NQ)

    def raw_src(e, k):
        if k < 4:
            w = (w1, w3)[k % 2]
            cols = slice(512 * (k // 2), 512 * (k // 2) + 512)
            return w[bass.ds(e, 1), :, cols].rearrange("e (i q) n -> i (e q) n", q=NQ)
        rows = slice(512 * (k - 4), 512 * (k - 4) + 512)
        return w2[bass.ds(e, 1), rows, :].rearrange("e (c p) n -> p (e c) n", p=P)

    with ExitStack() as ctx:
        def sb(name, shape, dt=F32, c=ctx):
            return c.enter_context(nc.sbuf_tensor(name, shape, dt))

        def sem(name):
            return ctx.enter_context(nc.semaphore(name))

        xn_dram = nc.dram_tensor("xn_rows", [NT * P, L], F32, kind="Internal").ap()
        y_dram = nc.dram_tensor("expert_rows", [TILES * P, L], F32, kind="Internal").ap()

        X = sb("X", [P, NB, NBLK, NQ, D])
        ident = sb("ident", [P, P])
        below = sb("below", [P, P])
        ones = sb("ones", [P, P])
        iota = sb("iota", [P, P])
        thresholds = sb("thresholds", [P, 16])
        rank8 = sb("rank8", [P, E])
        tokid = sb("tokid", [P, NT])
        gates = sb("gates", [P, 2, NT])
        slot_i = sb("slot_i", [P, 2, NT], I32)
        src_i = sb("src_i", [P, SLOT_TILES], I32)
        tile_expert = sb("tile_expert", [1, SLOT_TILES], I32)
        tile_last = sb("tile_last", [1, TILES], I32)
        release = sb("release", [1, E, UNITS], I32)

        with ExitStack() as s:
            xin = sb("xin", [P, 2, NQ, C], c=s)
            taps = [sb(f"taps{n}", [P, NBLK, v], c=s) for n, v in enumerate(LAGS)]
            mixw = sb("mixw", [D, NS * D], c=s)
            gatew = sb("gatew", [E, L], c=s)
            mix4 = sb("mix4", [D, NS, NQ, D], c=s)
            mixT = sb("mixT", [P, NS, D], c=s)
            same = sb("same", [P, P], c=s)
            wc = [sb(f"wc{n}", [P, NBLK, v, D], c=s) for n, v in enumerate(LAGS)]
            xs = sb("xs", [P, NBLK, NB, PAD + P], c=s)
        with ExitStack() as s:
            w_lo = sb("w_lo", [P, RING, 4, 512], F32R, c=s)
            w_hi = sb("w_hi", [P, RING, 4, 512], F32R, c=s)
        with ExitStack() as s:
            w_raw = sb("w_raw", [P, RING, 4, 512], c=s)
        with ExitStack() as s:
            yb = sb("yb", [P, 4, 2, L], c=s)
            res = sb("res", [P, 2, NQ, P], c=s)
            ot = sb("ot", [P, 2, NQ, C], c=s)
        sb("held", [P, RING * 4 * 512 * 2])
        with ExitStack() as s:
            cs = sb("cs", [P, 8, NB, P], c=s)
            xnb = sb("xnb", [P, 2, NQ, P], c=s)
            xnT = sb("xnT", [P, NQ, P], c=s)
            xc = sb("xc", [P, 2, NQ, P], c=s)
        with ExitStack() as s:
            RT = [sb(f"rt{n}", [P, NT, E], c=s) for n in range(12)]
            small = sb("small", [P, 10, 16], c=s)
            cmp = sb("cmp", [P, SLOT_TILES * E], c=s)
            ohr = sb("ohr", [P, 2, P], c=s)
            oht = sb("oht", [P, 2, SLOT_TILES], c=s)
            sl_i = sb("sl_i", [P, 2, 2 * NT], I32, c=s)
            sl_f = sb("sl_f", [P, 2, 2 * NT], c=s)
        with ExitStack() as s:
            h = sb("h", [P, 2, 512], c=s)
            hT_hi = sb("hT_hi", [P, 2, 4, P], F32R, c=s)
            hT_lo = sb("hT_lo", [P, 2, 4, P], F32R, c=s)
            xg = sb("xg", [P, NQ, P], c=s)
            xT_hi = sb("xT_hi", [P, NQ, P], F32R, c=s)
            xT_lo = sb("xT_lo", [P, NQ, P], F32R, c=s)
            y = sb("y", [P, L], c=s)
        sb("held2", [P, 26 * 256])
        gateT = sb("gateT", [P, NQ, E])
        bn6 = sb("bn6", [P, NBLK, 6])
        mom = sb("mom", [P, 6, NBLK])
        st6 = sb("st6", [P, 6])
        mv = sb("mv", [P, 2])
        rstd_t = sb("rstd_t", [P, 1])

        B = [ctx.enter_context(nc.psum_tensor(f"bank{n}", [P, 512], F32)) for n in range(8)]

        x_in = [sem(f"x_in{b}") for b in range(NB)]
        x_blocks = sem("x_blocks")
        taps_in, small_in = sem("taps_in"), sem("small_in")
        taps_zeroed, consts = sem("taps_zeroed"), sem("consts")
        pool_step, dve_step = sem("pool_step"), sem("dve_step")
        mix4_ready, small_ps, small_out = sem("mix4_ready"), sem("small_ps"), sem("small_out")
        xt_ps0, xs_out, pads = sem("xt_ps0"), sem("xs_out"), sem("pads")
        mom_ready, mom_ps = sem("mom_ready"), sem("mom_ps")
        var_in, sd_out = sem("var_in"), sem("sd_out")
        xs_norm, wc_ready = sem("xs_norm"), sem("wc_ready")
        conv_ps, conv_out = sem("conv_ps"), sem("conv_out")
        ct_ps, resid = sem("ct_ps"), sem("resid")
        tok_ps, tok_out, xn_ready = sem("tok_ps"), sem("tok_out"), sem("xn_ready")
        xn_st = [sem("xn_st0"), sem("xn_st1")]
        xnT_ps, xnT_out, logit_ps = sem("xnT_ps"), sem("xnT_out"), sem("logit_ps")
        ex_in, ex_out = sem("ex_in"), sem("ex_out")
        mask_ready, count_ps, onehot, src_ps = sem("mask_ready"), sem("count_ps"), sem("onehot"), sem("src_ps")
        routed = sem("routed")
        raw_in = [sem(f"raw_in{k}") for k in range(UNITS)]
        hi_ready, lo_ready = sem("hi_ready"), sem("lo_ready")
        xg_in, xg_ps, xT_hi_out, xT_lo_out = sem("xg_in"), sem("xg_ps"), sem("xT_hi_out"), sem("xT_lo_out")
        unit_done = sem("unit_done")
        silu_out, h_out, hT_ps, hT_hi_out, hT_lo_out = (sem("silu_out"), sem("h_out"), sem("hT_ps"),
                                                        sem("hT_hi_out"), sem("hT_lo_out"))
        y_out, y_st = sem("y_out"), sem("y_st")
        yb_in = [sem(f"yb_in{n}") for n in range(4)]
        res_out, res_ps, ot_out = sem("res_out"), sem("res_ps"), sem("ot_out")
        out_st = [sem("out_st0"), sem("out_st1")]

        CONSTS = 7

        STEPS = NBLK + 7

        def gb(n):
            return n // NB, n % NB

        def tokens(n):
            g, b = gb(n)
            return X[:, b, 4 * g:4 * g + 4, :, :].rearrange("p k q d -> p (k q d)")

        def col(n):
            g, b = gb(n)
            return NG * b + g

        def place(w, e, k):
            return w[:, bass.ds((e * UNITS + k) % RING, 1), :, :].rearrange("p o c n -> p (o c n)")

        def high_half(eng, e, k):
            eng.wait_ge(raw_in[k], (e + 1) * 16)
            eng.activation(place(w_hi, e, k), place(w_raw, e, k), ACT.Copy).then_inc(hi_ready, 1)

        def low_half(eng, e, k):
            eng.wait_ge(hi_ready, e * UNITS + (k + 1))
            eng.tensor_tensor(place(w_lo, e, k), place(w_raw, e, k), place(w_hi, e, k),
                              ALU.subtract).then_inc(lo_ready, 1)

        block = ctx.enter_context(nc.Block())

        @block.sync
        def _(sp):
            for b in range(NB):
                if b >= 2:
                    sp.wait_ge(x_blocks, b - 1)
                sp.dma_start(xin[:, b % 2, :, :], x_nat[b]).then_inc(x_in[b], 16)
            sp.wait_ge(x_blocks, NB)

            def load_unit(e, k):
                later = not isinstance(e, int)
                v = e * UNITS + k
                back, kk = divmod(UNITS * 2 + k - RING, UNITS)
                if later or e >= 1:
                    sp.wait_ge(lo_ready, v - (UNITS - 1))
                if later or e >= 2 - back:
                    sp.wait_ge(unit_done, sp.value_load(
                        release[0:1, bass.ds(e - (2 - back), 1), kk:kk + 1].rearrange("o e k -> o (e k)"),
                        min_val=1, max_val=UNITS * (TILES + 1)))
                sp.dma_start(w_raw[:, bass.ds(v % RING, 1), :, :].rearrange("p o c n -> p (o c) n"),
                             raw_src(e, k)).then_inc(raw_in[k], 16)

            for k in range(UNITS):
                if k == 2:
                    sp.wait_ge(conv_ps, NBLK)
                load_unit(0, k)
            for k in range(UNITS):
                if k == RING - UNITS:
                    sp.wait_ge(routed, 2)
                load_unit(1, k)
            with sp.Fori(2, E) as e:
                for k in range(UNITS):
                    load_unit(e, k)

            for b in range(NB):
                sp.wait_ge(ot_out, NG * (b + 1))
                sp.dma_start(out_nat[b], ot[:, b % 2, :, :]).then_inc(out_st[b % 2], 16)
            for n in range(2):
                sp.wait_ge(out_st[n], 16 * (NB // 2))

        @block.gpsimd
        def _(pool):
            steps = [0]

            def then_next(ins):
                steps[0] += 1
                ins.then_inc(pool_step, 1)
                pool.wait_ge(pool_step, steps[0])

            for n in range(NS):
                pool.memset(taps[n][:], 0.0).then_inc(taps_zeroed, 1)
            pool.memset(xs[:, :, :, 0:PAD], 0.0).then_inc(pads, 1)
            then_next(pool.memset(ident[:], 0.0))
            pool.affine_select(out=ident[:], in_=ident[:], compare_op=ALU.not_equal, fill=1.0, base=0,
                               pattern=[[-1, P]], channel_multiplier=1).then_inc(consts, 1)
            then_next(pool.memset(same[:], 0.0))
            for a in range(NQ):
                v = same[:].rearrange("p (q m) -> p q m", q=NQ)
                then_next(pool.affine_select(out=v, in_=v, compare_op=ALU.not_equal, fill=1.0 / NQ,
                                             base=-D * a, pattern=[[0, NQ], [-1, D]], channel_multiplier=1))
            pool.memset(ones[:], 1.0).then_inc(consts, 1)
            pool.wait_ge(consts, 2)
            pool.affine_select(out=below[:], in_=ones[:], compare_op=ALU.is_gt, fill=0.0, base=0,
                               pattern=[[1, P]], channel_multiplier=-1).then_inc(consts, 1)

            pool.wait_ge(taps_in, 16 * NQ * NS)
            pool.wait_ge(small_out, 2)
            for n, v in enumerate(LAGS):
                for j in range(NS):
                    b0 = (j - n) % NS
                    nb = len(range(b0, NBLK, NS))
                    pool.tensor_tensor(
                        wc[n][:, b0::NS, :, :],
                        taps[n][:, b0::NS, ::-1].unsqueeze(3).broadcast_to([P, nb, v, D]),
                        mixT[:, j, :].unsqueeze(1).unsqueeze(1).broadcast_to([P, nb, v, D]),
                        ALU.mult).then_inc(wc_ready, 1)
            flat = dict(allow_small_or_imprecise_dtypes=True)
            pool.iota(iota[:], pattern=[[1, P]], base=0, channel_multiplier=0, **flat).then_inc(consts, 1)
            pool.iota(thresholds[:], pattern=[[P, 16]], base=0, channel_multiplier=0, **flat).then_inc(consts, 1)
            pool.iota(rank8[:], pattern=[[-1, E]], base=E, channel_multiplier=0, **flat).then_inc(consts, 1)
            pool.iota(tokid[:], pattern=[[P, NT]], base=0, channel_multiplier=1, **flat).then_inc(consts, 1)

            for k in range(4):
                low_half(pool, 0, k)

            pool.wait_ge(routed, 2)
            for n in range(2):
                pool.wait_ge(xn_st[n], 16 * NT // 2)
            for t in range(SLOT_TILES):
                if t >= 1:
                    pool.wait_ge(xg_ps, t)
                pool.indirect_dma_start(
                    out=xg[:].rearrange("p q i -> p (q i)"), out_offset=None, in_=xn_dram,
                    in_offset=bass.IndirectOffsetOnAxis(ap=src_i[:, t:t + 1], axis=0),
                ).then_inc(xg_in, 16)

            pool.wait_ge(y_st, 16 * TILES)
            for n in range(NT):
                if n >= 4:
                    pool.wait_ge(res_out, n - 3)
                for j in range(2):
                    pool.indirect_dma_start(
                        out=yb[:, n % 4, j, :], out_offset=None, in_=y_dram,
                        in_offset=bass.IndirectOffsetOnAxis(ap=slot_i[:, j, n:n + 1], axis=0),
                    ).then_inc(yb_in[n % 4], 16)

        @block.scalar
        def _(act):
            act.dma_start(mixw[:], w_mix).then_inc(small_in, 16)
            act.dma_start(gatew[:], gate_w).then_inc(small_in, 16)
            act.wait_ge(taps_zeroed, NS)
            for n, k in enumerate(TAPS):
                src = taps_dram[n].rearrange("(blk m) o k -> m blk (o k)", m=D)
                for p in range(NQ):
                    at = LAGS[n] - k - p
                    act.dma_start(taps[n][D * p:D * p + D, :, at:at + k], src).then_inc(taps_in, 16)

            def deviation(b):
                act.wait_ge(var_in, b + 1)
                act.activation(mom[:, 3, :], mom[:, 3, :], ACT.Sqrt).then_inc(sd_out, 1)

            for n in range(NB * 4):
                b, k4 = n // 4, n % 4
                act.wait_ge(xt_ps0, n + 1)
                act.activation(xs[:, 4 * k4:4 * k4 + 4, b, PAD:], B[n % 4][:].rearrange("p (k i) -> p k i", i=P),
                               ACT.Copy).then_inc(xs_out, 1)
                if b >= 1 and k4 == 3:
                    deviation(b - 1)
            deviation(NB - 1)

            for i in range(STEPS):
                if i < NBLK:
                    act.wait_ge(conv_ps, i + 1)
                    if i >= 8:
                        act.wait_ge(ct_ps, 4 * (i // 4 - 1))
                    act.activation(cs[:, i % 8, :, :], B[i % 2][:].rearrange("p (b i) -> p b i", i=P),
                                   ACT.Copy).then_inc(conv_out, 1)
                n = i - 5
                if 0 <= n < NT:
                    act.wait_ge(tok_ps, n + 1)
                    act.activation(tokens(n), B[4 + n % 2][:], ACT.Copy).then_inc(tok_out, 1)
                    act.wait_ge(var_in, NB + n + 1)
                    act.activation(rstd_t[:], rstd_t[:], ACT.Sqrt).then_inc(sd_out, 1)
                n = i - 6
                if 0 <= n < NT:
                    act.wait_ge(xn_ready, n + 1)
                    act.dma_start(xn_dram[P * col(n):P * col(n) + P, :],
                                  xnb[:, n % 2, :, :].rearrange("p q i -> p (q i)")).then_inc(xn_st[n % 2], 16)
                    act.wait_ge(xnT_ps, n + 1)
                    if n >= 1:
                        act.wait_ge(logit_ps, n)
                    act.activation(xnT[:].rearrange("p q i -> p (q i)"), B[6][:], ACT.Copy).then_inc(xnT_out, 1)

            act.wait_ge(ex_in, 1)
            act.activation(RT[1][:], RT[1][:], ACT.Exp).then_inc(ex_out, 1)

            for k in range(UNITS):
                high_half(act, 0, k)
            act.wait_ge(xg_ps, 1)
            act.activation(xT_hi[:], B[6][:].rearrange("p (q i) -> p q i", i=P), ACT.Copy).then_inc(xT_hi_out, 1)

            def act_tile(t, first=False):
                e = act.value_load(tile_expert[0:1, bass.ds(t, 1)], min_val=0, max_val=E - 1)
                last = act.value_load(tile_last[0:1, bass.ds(t, 1)], min_val=0, max_val=1)

                def next_expert(*ks):
                    with act.If_ne(last.val, 0):
                        for k in ks:
                            high_half(act, e + 1, k)

                def silu(j):
                    act.wait_ge(unit_done, t * UNITS + (2 * j + 2))
                    if not first:
                        act.wait_ge(hT_ps, t * 2 + (j - 1))
                    act.activation(h[:, j, :], B[2 * j][:], ACT.Silu).then_inc(silu_out, 1)

                def hi(j):
                    act.wait_ge(hT_ps, t * 2 + (j + 1))
                    if not first:
                        act.wait_ge(unit_done, t * UNITS + j)
                    act.activation(hT_hi[:, j, :, :], B[4 + j][:].rearrange("p (c n) -> p c n", n=P),
                                   ACT.Copy).then_inc(hT_hi_out, 1)

                next_expert(0)
                silu(0)
                next_expert(1, 2)
                silu(1)
                hi(0)
                next_expert(3)
                act.wait_ge(xg_ps, t + 2)
                act.activation(xT_hi[:], B[6][:].rearrange("p (q i) -> p q i", i=P),
                               ACT.Copy).then_inc(xT_hi_out, 1)
                hi(1)
                next_expert(4)
                act.wait_ge(unit_done, t * UNITS + (UNITS + 1))
                if not first:
                    act.wait_ge(y_st, t * 16)
                act.activation(y[:], B[7][:], ACT.Copy).then_inc(y_out, 1)
                act.wait_ge(y_out, t + 1)
                act.dma_start(y_dram[bass.ds(t * P, P), :], y[:]).then_inc(y_st, 16)
                next_expert(5)

            act_tile(0, first=True)
            with act.Fori(1, TILES) as t:
                act_tile(t)

            for m in range(NT):
                b, g = m // NG, m % NG
                act.wait_ge(res_ps, m + 1)
                if b >= 2:
                    act.wait_ge(out_st[b % 2], 16 * (b // 2))
                act.activation(ot[:, b % 2, :, P * g:P * g + P], B[m % 2][:].rearrange("p (q n) -> p q n", n=P),
                               ACT.Copy).then_inc(ot_out, 1)

        @block.tensor
        def _(pe):
            pe.wait_ge(consts, 1)
            pe.wait_ge(mix4_ready, 1)
            for j in range(NS):
                pe.transpose(B[5][:, D * j:D * j + D], mix4[:, j, :, :].rearrange("d q m -> d (q m)"), ident[0:D, 0:D])
            for q in range(NQ):
                ins = pe.transpose(B[5][:, P + E * q:P + E * q + E], gatew[:, q::NQ], ident[0:E, 0:E])
            ins.then_inc(small_ps, 1)

            def moments(b, k):
                pe.wait_ge(mom_ready, 2 * b + k + 1)
                pe.matmul(B[4 + k][:, NBLK * b:NBLK * b + NBLK], same[:], mom[:, (0, 4)[k], :],
                          start=True, stop=True).then_inc(mom_ps, 1)

            pe.wait_ge(small_out, 2)
            pe.wait_ge(pool_step, 6)
            for b in range(NB):
                pe.wait_ge(x_blocks, b + 1)
                for k4 in range(4):
                    n = 4 * b + k4
                    if n >= 4:
                        pe.wait_ge(xs_out, n - 3)
                    for k in range(4):
                        ins = pe.transpose(B[n % 4][:, P * k:P * k + P],
                                           X[:, b, 4 * k4 + k, :, :].rearrange("p q d -> p (q d)"), ident[:])
                    ins.then_inc(xt_ps0, 1)
                if b >= 1:
                    moments(b - 1, 0)
                    moments(b - 1, 1)
            moments(NB - 1, 0)
            moments(NB - 1, 1)

            def conv(i):
                parts = []
                for j in range(NS):
                    n, blk = divmod(NS * i + j, NBLK)
                    parts += [(n, blk, d) for d in range(LAGS[n] // NQ)]
                pe.wait_ge(wc_ready, NS * (max(p[0] for p in parts) + 1))
                if i >= 2:
                    pe.wait_ge(conv_out, i - 1)
                for a, (n, blk, d) in enumerate(parts):
                    ins = pe.matmul(B[i % 2][:].rearrange("p (b i) -> p b i", i=P),
                                    wc[n][:, blk, NQ * d:NQ * d + NQ, :].rearrange("p v d -> p (v d)"),
                                    xs[:, blk, :, PAD - d:PAD - d + P],
                                    start=(a == 0), stop=(a == len(parts) - 1))
                ins.then_inc(conv_ps, 1)

            pe.wait_ge(xs_norm, NB)
            pe.wait_ge(pads, 1)
            for i in range(STEPS):
                if i < NBLK:
                    conv(i)
                n = i - 4
                if 0 <= n < NT:
                    g, b = gb(n)
                    pe.wait_ge(conv_out, 4 * g + 4)
                    if n >= 2:
                        pe.wait_ge(resid, n - 1)
                    for k in range(4):
                        ins = pe.transpose(B[2 + n % 2][:, P * k:P * k + P], cs[:, (4 * g + k) % 8, b, :], ident[:])
                    ins.then_inc(ct_ps, 1)
                n = i - 5
                if 0 <= n < NT:
                    g, b = gb(n)
                    pe.wait_ge(resid, n + 1)
                    if n >= 2:
                        pe.wait_ge(tok_out, n - 1)
                    for q in range(NQ):
                        ins = pe.transpose(B[4 + n % 2][:, P * q:P * q + P], xc[:, n % 2, q, :], ident[:])
                    ins.then_inc(tok_ps, 1)
                n = i - 6
                if 0 <= n < NT:
                    pe.wait_ge(xn_ready, n + 1)
                    if n >= 1:
                        pe.wait_ge(xnT_out, n)
                    for q in range(NQ):
                        ins = pe.transpose(B[6][:, P * q:P * q + P], xnb[:, n % 2, q, :], ident[:])
                    ins.then_inc(xnT_ps, 1)
                n = i - 7
                if 0 <= n < NT:
                    pe.wait_ge(xnT_out, n + 1)
                    for q in range(NQ):
                        ins = pe.matmul(B[7][:, E * col(n):E * col(n) + E], xnT[:, q, :], gateT[:, q, :],
                                        start=(q == 0), stop=(q == NQ - 1))
                    ins.then_inc(logit_ps, 1)

            pe.wait_ge(mask_ready, 1)
            pe.wait_ge(consts, CONSTS)
            masks = RT[6][:].rearrange("p t e -> p (t e)")
            pe.matmul(B[0][:, 0:P], below[:], masks, start=True, stop=True)
            pe.matmul(B[1][:, 0:P], ones[:], masks, start=True, stop=True).then_inc(count_ps, 1)
            for a in range(2 * NT):
                pe.wait_ge(onehot, a + 1)
                ins = pe.matmul(B[2][:, 0:SLOT_TILES], ohr[:, a % 2, :], oht[:, a % 2, :],
                                start=(a == 0), stop=(a == 2 * NT - 1))
                ins.then_inc(src_ps, 1)

            def turn_tokens(n):
                pe.wait_ge(xg_in, n * 16)
                for q in range(NQ):
                    ins = pe.transpose(B[6][:, P * q:P * q + P], xg[:, q, :], ident[:])
                ins.then_inc(xg_ps, 1)

            def product(bank, stat_hi, stat_lo, slot, c, start, stop):
                hi, lo = (w[:, bass.ds(slot, 1), c, :].rearrange("p o n -> p (o n)") for w in (w_hi, w_lo))
                pe.matmul(B[bank][:], stat_hi, hi, start=start, stop=False)
                pe.matmul(B[bank][:], stat_hi, lo, start=False, stop=False)
                return pe.matmul(B[bank][:], stat_lo, hi, start=False, stop=stop)

            def pe_tile(t, first=False):
                e = pe.value_load(tile_expert[0:1, bass.ds(t, 1)], min_val=0, max_val=E - 1)
                slots = []

                def weights(k):
                    v = pe.snap(e * UNITS + k)
                    pe.wait_ge(hi_ready, v + 1)
                    pe.wait_ge(lo_ready, v + 1)
                    return v % RING

                def up(k):
                    slot = weights(k)
                    if not first:
                        pe.wait_ge((silu_out, h_out)[k % 2], t * 2 + (k // 2 - 1))
                    for c in range(4):
                        ins = product(k, xT_hi[:, c, :], xT_lo[:, c, :], slot, c, c == 0, c == 3)
                    ins.then_inc(unit_done, 1)

                def turn_h(j):
                    pe.wait_ge(h_out, t * 2 + (j + 1))
                    if not first:
                        pe.wait_ge(hT_lo_out, t * 2 + (j - 1))
                    for c in range(4):
                        ins = pe.transpose(B[4 + j][:, P * c:P * c + P], h[:, j, P * c:P * c + P], ident[:])
                    ins.then_inc(hT_ps, 1)

                def down(j, chunks, slot):
                    for c in chunks:
                        ins = product(7, hT_hi[:, j, c, :], hT_lo[:, j, c, :], slot, c,
                                      j == 0 and c == 0, j == 1 and c == 3)
                    return ins

                pe.wait_ge(xT_hi_out, t + 1)
                pe.wait_ge(xT_lo_out, t + 1)
                up(0)
                up(1)
                up(2)
                turn_h(0)
                up(3)
                turn_tokens(t + 2)
                slot = weights(4)
                pe.wait_ge(hT_hi_out, t * 2 + 1)
                pe.wait_ge(hT_lo_out, t * 2 + 1)
                if not first:
                    pe.wait_ge(y_out, t)
                down(0, (0, 1), slot)
                turn_h(1)
                down(0, (2, 3), slot).then_inc(unit_done, 1)
                slot = weights(5)
                pe.wait_ge(hT_hi_out, t * 2 + 2)
                pe.wait_ge(hT_lo_out, t * 2 + 2)
                down(1, range(4), slot).then_inc(unit_done, 1)

            pe.wait_ge(routed, 2)
            pe.sem_inc(unit_done, 1)
            turn_tokens(1)
            pe_tile(0, first=True)
            with pe.Fori(1, TILES) as t:
                pe_tile(t)

            for m in range(NT):
                pe.wait_ge(res_out, m + 1)
                if m >= 2:
                    pe.wait_ge(ot_out, m - 1)
                for q in range(NQ):
                    ins = pe.transpose(B[m % 2][:, P * q:P * q + P], res[:, m % 2, q, :], ident[:])
                ins.then_inc(res_ps, 1)

        @block.vector
        def _(dve):
            steps = [0]

            def then_next(ins):
                steps[0] += 1
                ins.then_inc(dve_step, 1)
                dve.wait_ge(dve_step, steps[0])

            dve.wait_ge(small_in, 32)
            dve.tensor_copy(mix4[:], mixw[:].rearrange("d (j m) -> d j m", j=NS).unsqueeze(2)
                            .broadcast_to([D, NS, NQ, D])).then_inc(mix4_ready, 1)
            dve.wait_ge(small_ps, 1)
            dve.tensor_copy(mixT[:], B[5][:, 0:NS * D].rearrange("p (j d) -> p j d", d=D)).then_inc(small_out, 1)
            dve.tensor_copy(gateT[:], B[5][:, P:P + NQ * E].rearrange("p (q e) -> p q e", e=E)).then_inc(small_out, 1)

            mean, dm, var, dev, mean_all = (mom[:, k, :] for k in (0, 1, 2, 3, 5))
            def to_blocks(b):
                dve.wait_ge(x_in[b], 16)
                dve.tensor_copy(X[:, b, :, :, :], xin[:, b % 2, :, :].rearrange("p q (k d) -> p k q d", d=D)
                                ).then_inc(x_blocks, 1)

            to_blocks(0)
            for b in range(NB):
                if b + 1 < NB:
                    to_blocks(b + 1)
                for k in range(NBLK):
                    if k % 4 == 0:
                        dve.wait_ge(xs_out, 4 * b + k // 4 + 1)
                    ins = dve.bn_stats(bn6[:, k, :], xs[:, k, b, PAD:])
                then_next(ins)
                dve.tensor_tensor(mean, bn6[:, :, 1], bn6[:, :, 4], ALU.add)
                then_next(dve.tensor_tensor(dm, bn6[:, :, 1], bn6[:, :, 4], ALU.subtract))
                dve.tensor_scalar(mean, mean, 0.5, None, ALU.mult).then_inc(mom_ready, 1)
                dve.tensor_tensor(var, bn6[:, :, 2], bn6[:, :, 5], ALU.add)
                then_next(dve.tensor_tensor(dm, dm, dm, ALU.mult))
                then_next(dve.scalar_tensor_tensor(out=var, in0=dm, scalar=P / 4.0, in1=var, op0=ALU.mult, op1=ALU.add))
                dve.wait_ge(mom_ps, 2 * b + 1)
                then_next(dve.tensor_copy(mean_all, B[4][:, NBLK * b:NBLK * b + NBLK]))
                then_next(dve.tensor_tensor(dev, mean, mean_all, ALU.subtract))
                then_next(dve.tensor_tensor(dev, dev, dev, ALU.mult))
                dve.scalar_tensor_tensor(out=mom[:, 4, :], in0=var, scalar=1.0 / P, in1=dev,
                                         op0=ALU.mult, op1=ALU.add).then_inc(mom_ready, 1)
                dve.wait_ge(mom_ps, 2 * b + 2)
                dve.tensor_scalar(dev, B[5][:, NBLK * b:NBLK * b + NBLK], EPS_C, None, ALU.add).then_inc(var_in, 1)
                dve.wait_ge(sd_out, b + 1)
                then_next(dve.reciprocal(dev, dev))
                for k in range(NBLK):
                    ins = dve.tensor_scalar(xs[:, k, b, PAD:], xs[:, k, b, PAD:], mean_all[:, k:k + 1],
                                            dev[:, k:k + 1], ALU.subtract, ALU.mult)
                ins.then_inc(xs_norm, 1)

            for i in range(STEPS):
                n = i - 4
                if 0 <= n < NT:
                    g, b = gb(n)
                    dve.wait_ge(ct_ps, n + 1)
                    if n >= 2:
                        dve.wait_ge(tok_ps, n - 1)
                    dve.tensor_tensor(xc[:, n % 2, :, :].rearrange("p q (k d) -> p k q d", d=D),
                                      B[2 + n % 2][:].rearrange("p (k q d) -> p k q d", q=NQ, d=D),
                                      X[:, b, 4 * g:4 * g + 4, :, :], ALU.add).then_inc(resid, 1)
                n = i - 5
                if 0 <= n < NT:
                    dve.wait_ge(tok_out, n + 1)
                    then_next(dve.bn_stats(st6[:], tokens(n)))
                    then_next(dve.bn_aggr(mv[:], st6[:]))
                    dve.tensor_scalar(rstd_t[:], mv[:, 1:2], EPS_T, None, ALU.add).then_inc(var_in, 1)
                    dve.wait_ge(sd_out, NB + n + 1)
                    then_next(dve.reciprocal(rstd_t[:], rstd_t[:]))
                    if n >= 2:
                        dve.wait_ge(xn_st[n % 2], 16 * (n // 2))
                        dve.wait_ge(xnT_ps, n - 1)
                    dve.tensor_scalar(xnb[:, n % 2, :, :].rearrange("p q i -> p (q i)"), tokens(n), mv[:, 0:1], rstd_t[:],
                                      ALU.subtract, ALU.mult).then_inc(xn_ready, 1)

            lg, ex, p, m1, m2, rest, both, before, base, sel = (RT[k][:] for k in range(10))
            scan = (RT[10][:], RT[11][:])

            def wide(v):
                return v.unsqueeze(2).broadcast_to([P, NT, E])

            ranks = rank8[:].unsqueeze(1).broadcast_to([P, NT, E])
            top, total, rsum, p1, p2, psum2, pick = (small[:, k, :] for k in range(7))
            cnt, ntile, end = (small[:, 7 + k, 0:E] for k in range(3))
            start_t = small[:, 7, E:2 * E]

            dve.wait_ge(logit_ps, NT)
            dve.wait_ge(consts, CONSTS)
            then_next(dve.tensor_copy(lg, B[7][:, 0:NT * E].rearrange("p (t e) -> p t e", e=E)))
            then_next(dve.tensor_reduce(top, lg, AX_X, ALU.max))
            dve.tensor_tensor(ex, lg, wide(top), ALU.subtract).then_inc(ex_in, 1)

            def pick_first(values, biggest, mask):
                then_next(dve.tensor_tensor(sel, values, wide(biggest), ALU.is_equal))
                then_next(dve.tensor_tensor(sel, sel, ranks, ALU.mult))
                then_next(dve.tensor_reduce(pick, sel, AX_X, ALU.max))
                then_next(dve.tensor_tensor(mask, ranks, wide(pick), ALU.is_equal))

            pick_first(lg, top, m1)
            then_next(dve.scalar_tensor_tensor(out=rest, in0=m1, scalar=-3.0e38, in1=lg, op0=ALU.mult, op1=ALU.add))
            then_next(dve.tensor_reduce(top, rest, AX_X, ALU.max))
            pick_first(rest, top, m2)
            dve.tensor_tensor(both, m1, m2, ALU.add).then_inc(mask_ready, 1)

            dve.wait_ge(ex_out, 1)
            then_next(dve.tensor_reduce(total, ex, AX_X, ALU.add))
            then_next(dve.reciprocal(rsum, total))
            then_next(dve.tensor_tensor(p, ex, wide(rsum), ALU.mult))
            for mask, pk in ((m1, p1), (m2, p2)):
                then_next(dve.tensor_tensor(sel, p, mask, ALU.mult))
                then_next(dve.tensor_reduce(pk, sel, AX_X, ALU.add))
            then_next(dve.tensor_tensor(psum2, p1, p2, ALU.add))
            then_next(dve.reciprocal(psum2, psum2))
            dve.tensor_tensor(gates[:, 0, :], p1, psum2, ALU.mult)
            then_next(dve.tensor_tensor(gates[:, 1, :], p2, psum2, ALU.mult))

            dve.wait_ge(count_ps, 1)
            whole = B[1][:, 0:NT * E].rearrange("p (t e) -> p t e", e=E)
            dve.memset(scan[0][:, 0:1, :], 0.0)
            then_next(dve.tensor_copy(scan[0][:, 1:, :], whole[:, 0:NT - 1, :]))
            a = 0
            for sft in (1, 2, 4, 8):
                dve.tensor_copy(scan[1 - a][:, 0:sft, :], scan[a][:, 0:sft, :])
                then_next(dve.tensor_tensor(scan[1 - a][:, sft:, :], scan[a][:, sft:, :],
                                            scan[a][:, 0:NT - sft, :], ALU.add))
                a = 1 - a
            then_next(dve.tensor_tensor(cnt, scan[a][:, NT - 1, :], whole[:, NT - 1, :], ALU.add))
            over = cmp[:, 0:E * 16].rearrange("p (e k) -> p e k", k=16)
            then_next(dve.tensor_tensor(over, cnt.unsqueeze(2).broadcast_to([P, E, 16]),
                                        thresholds[:].unsqueeze(1).broadcast_to([P, E, 16]), ALU.is_gt))
            then_next(dve.tensor_reduce(ntile, over, AX_X, ALU.add))
            then_next(dve.tensor_scalar(ntile, ntile, 1.0, None, ALU.max))
            then_next(dve.tensor_copy(end, ntile))
            for e in range(1, E):
                then_next(dve.tensor_tensor(end[:, e:e + 1], end[:, e:e + 1], end[:, e - 1:e], ALU.add))
            then_next(dve.tensor_tensor(start_t, end, ntile, ALU.subtract))
            then_next(dve.tensor_tensor(before, B[0][:, 0:NT * E].rearrange("p (t e) -> p t e", e=E), scan[a], ALU.add))
            then_next(dve.scalar_tensor_tensor(out=base, in0=start_t.unsqueeze(1).broadcast_to([P, NT, E]),
                                               scalar=float(P), in1=before, op0=ALU.mult, op1=ALU.add))
            for j, mask in enumerate((m1, m2)):
                then_next(dve.tensor_tensor(sel, base, mask, ALU.mult))
                then_next(dve.tensor_reduce(p1, sel, AX_X, ALU.add))
                then_next(dve.tensor_copy(sl_i[:, 1, NT * j:NT * j + NT], p1))
                dve.tensor_copy(slot_i[:, j, :], p1)
            then_next(dve.tensor_scalar(sl_i[:, 0, :], sl_i[:, 1, :], 7, None, ALU.arith_shift_right))
            then_next(dve.tensor_copy(sl_f[:, 0, :], sl_i[:, 0, :]))
            then_next(dve.tensor_scalar(sl_i[:, 0, :], sl_i[:, 1, :], P - 1, None, ALU.bitwise_and))
            then_next(dve.tensor_copy(sl_f[:, 1, :], sl_i[:, 0, :]))
            for a in range(2 * NT):
                if a >= 2:
                    dve.wait_ge(src_ps, a - 1)
                dve.tensor_scalar(ohr[:, a % 2, :], iota[:], sl_f[:, 1, a:a + 1], None, ALU.is_equal)
                dve.tensor_scalar(oht[:, a % 2, :], iota[:, 0:SLOT_TILES], sl_f[:, 0, a:a + 1],
                                  tokid[:, a % NT:a % NT + 1], ALU.is_equal, ALU.mult).then_inc(onehot, 1)
            passed = cmp[0:1, :].rearrange("p (t e) -> p t e", e=E)
            then_next(dve.tensor_tensor(passed, iota[0:1, 0:SLOT_TILES].unsqueeze(2).broadcast_to([1, SLOT_TILES, E]),
                                        end[0:1, :].unsqueeze(1).broadcast_to([1, SLOT_TILES, E]), ALU.is_ge))
            te = sl_f[0:1, :, :].rearrange("p a n -> p (a n)")[:, 0:SLOT_TILES]
            then_next(dve.tensor_reduce(te, passed, AX_X, ALU.add))
            then_next(dve.tensor_scalar(te, te, float(E - 1), None, ALU.min))
            then_next(dve.tensor_copy(tile_expert[:], te))
            dve.tensor_tensor(tile_last[:], te[:, 1:], te[:, 0:TILES], ALU.subtract)
            ends = cmp[0:1, 0:E]
            upto = cmp[0:1, E:E + E * UNITS].rearrange("p (e k) -> p e k", k=UNITS)
            then_next(dve.tensor_scalar(ends, end[0:1, :], float(UNITS), 2.0 - UNITS, ALU.mult, ALU.add))
            then_next(dve.tensor_tensor(upto, ends.unsqueeze(2).broadcast_to([1, E, UNITS]),
                                        iota[0:1, 0:UNITS].unsqueeze(1).broadcast_to([1, E, UNITS]), ALU.add))
            dve.tensor_scalar(release[:], upto, 1.0, None, ALU.max).then_inc(routed, 1)
            dve.wait_ge(src_ps, 2 * NT)
            dve.tensor_copy(src_i[:], B[2][:, 0:SLOT_TILES]).then_inc(routed, 1)

            def xT_rest(n):
                dve.wait_ge(xT_hi_out, n)
                dve.tensor_tensor(xT_lo[:], B[6][:].rearrange("p (q i) -> p q i", i=P), xT_hi[:],
                                  ALU.subtract).then_inc(xT_lo_out, 1)

            def dve_tile(t):
                e = dve.value_load(tile_expert[0:1, bass.ds(t, 1)], min_val=0, max_val=E - 1)
                last = dve.value_load(tile_last[0:1, bass.ds(t, 1)], min_val=0, max_val=1)

                def next_expert(*ks):
                    with dve.If_ne(last.val, 0):
                        for k in ks:
                            low_half(dve, e + 1, k)

                def gate_up(j):
                    dve.wait_ge(silu_out, t * 2 + (j + 1))
                    dve.wait_ge(unit_done, t * UNITS + (2 * j + 3))
                    dve.tensor_tensor(h[:, j, :], B[2 * j + 1][:], h[:, j, :], ALU.mult).then_inc(h_out, 1)

                def rest_of_hT(j):
                    dve.wait_ge(hT_hi_out, t * 2 + (j + 1))
                    dve.tensor_tensor(hT_lo[:, j, :, :], B[4 + j][:].rearrange("p (c n) -> p c n", n=P),
                                      hT_hi[:, j, :, :], ALU.subtract).then_inc(hT_lo_out, 1)

                next_expert(0)
                gate_up(0)
                next_expert(1, 2)
                rest_of_hT(0)
                gate_up(1)
                next_expert(3)
                xT_rest(t + 2)
                rest_of_hT(1)
                next_expert(4, 5)

            xT_rest(1)
            dve.wait_ge(lo_ready, 4)
            for k in range(4, UNITS):
                low_half(dve, 0, k)
            dve_tile(0)
            with dve.Fori(1, TILES) as t:
                dve_tile(t)

            for m in range(NT):
                b, g = m // NG, m % NG
                dve.wait_ge(yb_in[m % 4], 32 * (m // 4 + 1))
                if m >= 2:
                    dve.wait_ge(res_ps, m - 1)
                r = res[:, m % 2, :, :]
                rows = [yb[:, m % 4, j, :].rearrange("p (i q) -> p q i", q=NQ) for j in range(2)]
                then_next(dve.scalar_tensor_tensor(out=r, in0=rows[0], scalar=gates[:, 0, m:m + 1],
                                                   in1=tokens(NB * g + b).rearrange("p (q i) -> p q i", q=NQ), op0=ALU.mult, op1=ALU.add))
                dve.scalar_tensor_tensor(out=r, in0=rows[1], scalar=gates[:, 1, m:m + 1], in1=r,
                                         op0=ALU.mult, op1=ALU.add).then_inc(res_out, 1)


_INS = ["x", "L0_conv_w3", "L0_conv_w7", "L0_conv_w15", "L0_conv_w_mix", "L0_ffn_gate_w",
        "L0_ffn_w1", "L0_ffn_w2", "L0_ffn_w3"]


def kernel(**inputs):
    import numpy as _np
    import concourse.bacc as _bacc
    from concourse import mybir as _mybir
    from concourse.bass_utils import run_bass_kernel_spmd as _run

    nc = _bacc.Bacc("TRN2", target_bir_lowering=False, num_devices=1)
    arrays, args = {}, []
    for name in _INS:
        a = _np.ascontiguousarray(inputs[name])
        arrays[f"in_{name}"] = a
        args.append(nc.dram_tensor(f"in_{name}", a.shape, _mybir.dt.from_np(a.dtype), kind="ExternalInput").ap())
    args.append(nc.dram_tensor("out_x", inputs["x"].shape, F32, kind="ExternalOutput").ap())
    metaformer(nc, *args)
    r = _run(nc, [arrays], core_ids=[0])
    return r.results[0]["out_x"]
```

```python
from contextlib import ExitStack

import concourse.bass as bass
from concourse import mybir

F32 = mybir.dt.float32
F32R = mybir.dt.float32r
I32 = mybir.dt.int32
ALU = mybir.AluOpType
ACT = mybir.ActivationFunctionType
AX_X = mybir.AxisListType.X

P = 128
NB = 4
L = 512
C = 512
NQ = L // P
D = 32
NBLK = C // D
TAPS = (3, 7, 15)
NS = len(TAPS)
LAGS = tuple(NQ * -(-(k + NQ - 1) // NQ) for k in TAPS)
PAD = max(LAGS) // NQ - 1
CHUNKS = NS * max(LAGS) // NQ
WB = 3
XB = 4
NG = C // P
NT = NB * NG
E = 8
HID = 1024
TILES = NT * 2 + E - 1
SLOT_TILES = TILES + 1
POOL_UNITS = 5
UNITS = 6
TOKENS = NT * P
EPS_C = 1e-6
EPS_T = 1e-5


def metaformer(nc, x, w3c, w7c, w15c, w_mix, gate_w, w1, w2, w3, out):
    taps_dram = (w3c, w7c, w15c)
    x_nat = x.rearrange("b (i q) h w -> b i q (h w)", q=NQ)
    out_nat = out.rearrange("b (i q) h w -> b i q (h w)", q=NQ)

    def raw_src(e, k):
        if k < 4:
            w = (w1, w3)[k % 2]
            cols = slice(512 * (k // 2), 512 * (k // 2) + 512)
            return w[bass.ds(e, 1), :, cols].rearrange("e (i q) n -> i (e q) n", q=NQ)
        rows = slice(512 * (k - 4), 512 * (k - 4) + 512)
        return w2[bass.ds(e, 1), rows, :].rearrange("e (c p) n -> p (e c) n", p=P)

    with ExitStack() as ctx:
        def sb(name, shape, dt=F32, c=ctx):
            return c.enter_context(nc.sbuf_tensor(name, shape, dt))

        def sem(name):
            return ctx.enter_context(nc.semaphore(name))

        xn_dram = nc.dram_tensor("xn_rows", [TOKENS, L], F32, kind="Internal").ap()
        acc_dram = nc.dram_tensor("acc_rows", [TOKENS + P, L], F32, kind="Internal").ap()

        ident = sb("ident", [P, P])
        below = sb("below", [P, P])
        ones = sb("ones", [P, P])
        iota = sb("iota", [P, P])
        thresholds = sb("thresholds", [P, 16])
        rank8 = sb("rank8", [P, E])
        tokid = sb("tokid", [P, NT])
        spare = sb("spare", [P, SLOT_TILES])
        gates = sb("gates", [P, 2, NT])
        src_i = sb("src_i", [P, SLOT_TILES], I32)
        dst_i = sb("dst_i", [P, SLOT_TILES], I32)
        slot_gate = sb("slot_gate", [P, SLOT_TILES])
        gather_at = sb("gather_at", [P, 1], I32)
        add_at = sb("add_at", [P, 1], I32)
        tile_units = sb("tile_units", [1, TILES], I32)
        tile_last = sb("tile_last", [1, TILES], I32)

        with ExitStack() as s:
            X = sb("X", [P, NB, NBLK, NQ, D], c=s)
        with ExitStack() as s:
            RT = [sb(f"rt{n}", [P, NT, E], c=s) for n in range(12)]
            small = sb("small", [P, 10, 16], c=s)
            cmp = sb("cmp", [P, SLOT_TILES * E], c=s)
            sl_i = sb("sl_i", [P, 2, 2 * NT], I32, c=s)
            sl_f = sb("sl_f", [P, 2, 2 * NT], c=s)
            ohr = sb("ohr", [P, 2, P], c=s)
        with ExitStack() as s:
            sb("held0", [P, 2048 * 2], c=s)
            oht = sb("oht", [P, 2 * NT, 2, SLOT_TILES], c=s)
        sb("held1", [P, NB * NBLK * P])
        with ExitStack() as s:
            xc = sb("xc", [P, 2, NQ, P], c=s)
            xnT = sb("xnT", [P, NQ, P], c=s)
            xs = sb("xs", [P, NBLK, NB, PAD + P], c=s)
            xs_hi = sb("xs_hi", [P, NBLK, NB, PAD + P], F32R, c=s)
            wc = sb("wc", [P, WB, CHUNKS * P], c=s)
            wc_hi = sb("wc_hi", [P, WB, CHUNKS * P], F32R, c=s)
            taps = [sb(f"taps{n}", [P, NBLK, v], c=s) for n, v in enumerate(LAGS)]
            mixT = sb("mixT", [P, NS, D], c=s)
            xin = sb("xin", [P, 2, NB, NQ, P], c=s)
            taps_nat = [sb(f"taps_nat{n}", [D, NBLK, k], c=s) for n, k in enumerate(TAPS)]
            copies = sb("copies", [D, NQ, D], c=s)
            mixw = sb("mixw", [D, NS * D], c=s)
            gatew = sb("gatew", [E, L], c=s)
            mix4 = sb("mix4", [D, NS, NQ, D], c=s)
            same = sb("same", [P, P], c=s)
        with ExitStack() as s:
            sb("held_xc", [P, 3 * NQ * P], c=s)
            xs_lo = sb("xs_lo", [P, NBLK, NB, PAD + P], F32R, c=s)
            sb("held_xs_hi", [P, NBLK, NB, PAD + P], c=s)
            wc_lo = sb("wc_lo", [P, WB, CHUNKS * P], F32R, c=s)
        with ExitStack() as s:
            w_lo = sb("w_lo", [P, UNITS, 4, 512], F32R, c=s)
            w_hi = sb("w_hi", [P, UNITS, 4, 512], F32R, c=s)
            w_raw = sb("w_raw", [P, UNITS, 4, 512], c=s)
        with ExitStack() as s:
            rows = sb("rows", [P, 2, NG, L], c=s)
            ot = sb("ot", [P, 2, NQ, C], c=s)
        sb("held2", [P, 3 * UNITS * 4 * 512])
        with ExitStack() as s:
            cs = sb("cs", [P, 8, NB, P], c=s)
            xnb = sb("xnb", [P, XB, NQ, P], c=s)
        with ExitStack() as s:
            h = sb("h", [P, 2, 512], c=s)
            hT_hi = sb("hT_hi", [P, 2, 4, P], F32R, c=s)
            hT_lo = sb("hT_lo", [P, 2, 4, P], F32R, c=s)
            xg = sb("xg", [P, NQ, P], c=s)
            xT_hi = sb("xT_hi", [P, NQ, P], F32R, c=s)
            xT_lo = sb("xT_lo", [P, NQ, P], F32R, c=s)
            y = sb("y", [P, L], c=s)
        sb("held3", [P, 26 * 256])
        gateT = sb("gateT", [P, NQ, E])
        bn6 = sb("bn6", [P, NBLK, 6])
        mom = sb("mom", [P, 2, 6, NBLK])
        st6 = sb("st6", [P, 6])
        mv = sb("mv", [P, 2])
        rstd_t = sb("rstd_t", [P, 1])

        B = [ctx.enter_context(nc.psum_tensor(f"bank{n}", [P, 512], F32)) for n in range(8)]

        x_in = [sem(f"x_in{c}") for c in range(NG)]
        x_blocks = sem("x_blocks")
        taps_in, small_in = sem("taps_in"), sem("small_in")
        copies_ready, taps_ps, taps_out = sem("copies_ready"), sem("taps_ps"), sem("taps_out")
        taps_zeroed, consts = sem("taps_zeroed"), sem("consts")
        pool_step, dve_step = sem("pool_step"), sem("dve_step")
        mix4_ready, small_ps, small_out = sem("mix4_ready"), sem("small_ps"), sem("small_out")
        xt_ps0, xs_out, pads = sem("xt_ps0"), sem("xs_out"), sem("pads")
        mom_ready, mom_ps = sem("mom_ready"), sem("mom_ps")
        var_in, sd_out = sem("var_in"), sem("sd_out")
        xs_norm, xs_hi_out, xs_lo_out = sem("xs_norm"), sem("xs_hi_out"), sem("xs_lo_out")
        last_lo_out = sem("last_lo_out")
        wc_ready, wc_hi_out, wc_lo_out = sem("wc_ready"), sem("wc_hi_out"), sem("wc_lo_out")
        conv_ps, conv_out = sem("conv_ps"), sem("conv_out")
        ct_ps, resid = sem("ct_ps"), sem("resid")
        tok_ps, tok_out, xn_ready = sem("tok_ps"), sem("tok_out"), sem("xn_ready")
        xn_st = [sem(f"xn_st{n}") for n in range(XB)]
        acc_st = [sem(f"acc_st{b}") for b in range(NB)]
        spare_st = sem("spare_st")
        gather_index, add_index = sem("gather_index"), sem("add_index")
        xnT_ps, xnT_out, logit_ps = sem("xnT_ps"), sem("xnT_out"), sem("logit_ps")
        ex_in, ex_out = sem("ex_in"), sem("ex_out")
        mask_ready, count_ps, onehot, src_ps = sem("mask_ready"), sem("count_ps"), sem("onehot"), sem("src_ps")
        routed = sem("routed")
        raw_in = [sem(f"raw_in{k}") for k in range(UNITS)]
        hi_ready, lo_ready = sem("hi_ready"), sem("lo_ready")
        xg_in, xg_ps, xT_hi_out, xT_lo_out = sem("xg_in"), sem("xg_ps"), sem("xT_hi_out"), sem("xT_lo_out")
        unit_done = sem("unit_done")
        silu_out, h_out, hT_ps, hT_hi_out, hT_lo_out = (sem("silu_out"), sem("h_out"), sem("hT_ps"),
                                                        sem("hT_hi_out"), sem("hT_lo_out"))
        y_out, y_st = sem("y_out"), sem("y_st")
        all_added = sem("all_added")
        rows_in = [sem("rows_in0"), sem("rows_in1")]
        rows_ps, ot_out = sem("rows_ps"), sem("ot_out")
        out_st = [sem("out_st0"), sem("out_st1")]

        CONSTS = 8

        STEPS = NBLK + 7

        def gb(n):
            return n // NB, n % NB

        def tokens(n):
            g, b = gb(n)
            return X[:, b, 4 * g:4 * g + 4, :, :].rearrange("p k q d -> p (k q d)")

        def col(n):
            g, b = gb(n)
            return NG * b + g

        def high_half(eng, e, k):
            eng.wait_ge(raw_in[k], (e + 1) * 16)
            eng.activation(w_hi[:, k, :, :], w_raw[:, UNITS - 1 - k, :, :], ACT.Copy).then_inc(hi_ready, 1)

        def low_half(eng, e, k):
            eng.wait_ge(hi_ready, e * UNITS + (k + 1))
            eng.tensor_tensor(w_lo[:, k, :, :], w_raw[:, UNITS - 1 - k, :, :], w_hi[:, k, :, :],
                              ALU.subtract).then_inc(lo_ready, 1)

        def taps_view(n):
            at = NBLK * sum(TAPS[:n])
            return B[4][:, at:at + NBLK * TAPS[n]]

        def head_parts(i):
            return [(*divmod(NS * i + j, NBLK), j) for j in range(NS)]

        def head_columns(i):
            return sum(LAGS[n] * D for n, _, _ in head_parts(i))

        def wc_low(eng, i):
            cols = slice(0, head_columns(i))
            eng.wait_ge(wc_hi_out, i + 1)
            eng.tensor_tensor(wc_lo[:, i % WB, cols], wc[:, i % WB, cols], wc_hi[:, i % WB, cols],
                              ALU.subtract).then_inc(wc_lo_out, 1)

        def x_low(eng, c):
            eng.wait_ge(xs_hi_out, c + 1)
            blocks = slice(4 * c, 4 * c + 4)
            eng.tensor_tensor(xs_lo[:, blocks, :, :], xs[:, blocks, :, :], xs_hi[:, blocks, :, :],
                              ALU.subtract).then_inc(xs_lo_out if c < NG - 1 else last_lo_out, 1)

        EARLY = 5

        block = ctx.enter_context(nc.Block())

        @block.sync
        def _(sp):
            for c in range(NG):
                if c >= 2:
                    sp.wait_ge(x_blocks, NB * (c - 1))
                for b in range(NB):
                    sp.dma_start(xin[:, c % 2, b, :, :], x_nat[b][:, :, P * c:P * c + P]).then_inc(x_in[c], 16)

            def load_unit(e, k):
                sp.dma_start(w_raw[:, UNITS - 1 - k, :, :], raw_src(e, k)).then_inc(raw_in[k], 16)

            sp.wait_ge(x_blocks, NB * NG)
            sp.wait_ge(mom_ps, 2 * NG)
            for k in range(UNITS):
                if k == 3:
                    sp.wait_ge(conv_ps, NBLK)
                load_unit(0, k)
            with sp.Fori(1, E) as e:
                for k in range(UNITS):
                    sp.wait_ge(lo_ready, e * UNITS + (k + 1 - UNITS))
                    load_unit(e, k)

            sp.wait_ge(all_added, 1)
            def load_rows(b):
                sp.dma_start(rows[:, b % 2, :, :], acc_dram[C * b:C * b + C, :].rearrange("(g p) l -> p g l", p=P)
                             ).then_inc(rows_in[b % 2], 16)

            load_rows(0)
            load_rows(1)
            for b in range(NB):
                sp.wait_ge(ot_out, NG * (b + 1))
                sp.dma_start(out_nat[b], ot[:, b % 2, :, :]).then_inc(out_st[b % 2], 16)
                if b + 2 < NB:
                    load_rows(b + 2)
            for n in range(2):
                sp.wait_ge(out_st[n], 16 * (NB // 2))

        @block.gpsimd
        def _(pool):
            steps = [0]

            def then_next(ins):
                steps[0] += 1
                ins.then_inc(pool_step, 1)
                pool.wait_ge(pool_step, steps[0])

            for n in range(NS):
                pool.memset(taps[n][:], 0.0).then_inc(taps_zeroed, 1)
            pool.memset(xs[:, :, :, 0:PAD], 0.0).then_inc(pads, 1)
            then_next(pool.memset(ident[:], 0.0))
            pool.affine_select(out=ident[:], in_=ident[:], compare_op=ALU.not_equal, fill=1.0, base=0,
                               pattern=[[-1, P]], channel_multiplier=1).then_inc(consts, 1)
            then_next(pool.memset(same[:], 0.0))
            for a in range(NQ):
                v = same[:].rearrange("p (q m) -> p q m", q=NQ)
                then_next(pool.affine_select(out=v, in_=v, compare_op=ALU.not_equal, fill=1.0 / NQ,
                                             base=-D * a, pattern=[[0, NQ], [-1, D]], channel_multiplier=1))
            pool.memset(ones[:], 1.0).then_inc(consts, 1)
            pool.wait_ge(consts, 2)
            pool.affine_select(out=below[:], in_=ones[:], compare_op=ALU.is_gt, fill=0.0, base=0,
                               pattern=[[1, P]], channel_multiplier=-1).then_inc(consts, 1)

            def multiply_taps(i):
                if i >= WB:
                    pool.wait_ge(conv_ps, i - WB + 1)
                parts, at = head_parts(i), 0
                for n in sorted({p[0] for p in parts}):
                    run = [p for p in parts if p[0] == n]
                    nb, v, blk, j = len(run), LAGS[n], run[0][1], run[0][2]
                    ins = pool.tensor_tensor(
                        wc[:, i % WB, at:at + nb * v * D].rearrange("p (b v d) -> p b v d", b=nb, v=v),
                        taps[n][:, blk:blk + nb, ::-1].unsqueeze(3).broadcast_to([P, nb, v, D]),
                        mixT[:, j:j + nb, :].unsqueeze(2).broadcast_to([P, nb, v, D]), ALU.mult)
                    at += nb * v * D
                ins.then_inc(wc_ready, 1)

            pool.wait_ge(taps_out, NS * NQ)
            pool.wait_ge(small_out, 2)
            for i in range(WB):
                multiply_taps(i)
            for i in range(WB):
                wc_low(pool, i)
            x_low(pool, 0)
            x_low(pool, 1)
            multiply_taps(WB)
            wc_low(pool, WB)
            x_low(pool, 2)
            multiply_taps(WB + 1)
            wc_low(pool, WB + 1)
            for i in range(EARLY, NBLK):
                multiply_taps(i)
            flat = dict(allow_small_or_imprecise_dtypes=True)
            pool.iota(iota[:], pattern=[[1, P]], base=0, channel_multiplier=0, **flat).then_inc(consts, 1)
            pool.iota(thresholds[:], pattern=[[P, 16]], base=0, channel_multiplier=0, **flat).then_inc(consts, 1)
            pool.iota(rank8[:], pattern=[[-1, E]], base=E, channel_multiplier=0, **flat).then_inc(consts, 1)
            pool.iota(spare[:], pattern=[[0, SLOT_TILES]], base=TOKENS + 1, channel_multiplier=1,
                      **flat).then_inc(consts, 1)
            pool.iota(tokid[:], pattern=[[P, NT]], base=1, channel_multiplier=1, **flat).then_inc(consts, 1)

            pool.wait_ge(logit_ps, NT)
            for k in range(POOL_UNITS):
                low_half(pool, 0, k)

            def gather():
                pool.indirect_dma_start(
                    out=xg[:].rearrange("p q i -> p (q i)"), out_offset=None, in_=xn_dram,
                    in_offset=bass.IndirectOffsetOnAxis(ap=gather_at[:, 0:1], axis=0)).then_inc(xg_in, 16)

            def pool_tile(t, t1, added):
                pool.wait_ge(xg_ps, t1)
                pool.wait_ge(routed, 2)
                pool.tensor_copy(gather_at[:], src_i[:, bass.ds(t1, 1)]).then_inc(gather_index, 1)
                pool.wait_ge(xn_st[XB - 1], 16 * NT // XB)
                pool.wait_ge(gather_index, t1)
                gather()
                pool.tensor_copy(add_at[:], dst_i[:, bass.ds(t, 1)]).then_inc(add_index, 1)
                pool.wait_ge(spare_st, 16)
                pool.wait_ge(add_index, t1)
                pool.wait_ge(y_out, t1)
                pool.indirect_dma_start(
                    out=acc_dram, out_offset=bass.IndirectOffsetOnAxis(ap=add_at[:, 0:1], axis=0),
                    in_=y[:], in_offset=None, compute_op=ALU.add).then_inc(y_st, 16)
                pool.wait_ge(y_st, added)

            for n in range(XB):
                pool.wait_ge(xn_st[n], 16 * NT // XB)
            for b in range(NB):
                pool.wait_ge(acc_st[b], 16 * NG)
            pool.wait_ge(routed, 2)
            then_next(pool.tensor_copy(gather_at[:], src_i[:, 0:1]))
            gather()
            pool_tile(0, 1, 16)
            with pool.Fori(1, TILES) as t:
                live = pool.value_load(tile_units[0:1, bass.ds(t, 1)], min_val=0, max_val=UNITS * E)
                with pool.If_ne(live.val, 0):
                    pool_tile(t, pool.snap(t + 1), pool.snap(t * 16 + 16))
                    pool.nop()
            pool.sem_inc(all_added, 1)

        @block.scalar
        def _(act):
            act.dma_start(mixw[:], w_mix).then_inc(small_in, 16)
            act.dma_start(gatew[:], gate_w).then_inc(small_in, 16)
            for n in range(NS):
                act.dma_start(taps_nat[n][:], taps_dram[n].rearrange("(blk m) o k -> m blk (o k)", m=D)
                              ).then_inc(taps_in, 16)

            def x_turned(c):
                for b in range(NB):
                    act.wait_ge(xt_ps0, NB * c + b + 1)
                    act.activation(xs[:, 4 * c:4 * c + 4, b, PAD:], B[2 + b][:].rearrange("p (k i) -> p k i", i=P),
                                   ACT.Copy).then_inc(xs_out, 1)

            def deviation(c):
                act.wait_ge(var_in, c + 1)
                act.activation(mom[:, c % 2, 3, :], mom[:, c % 2, 3, :], ACT.Sqrt).then_inc(sd_out, 1)

            def x_high(c):
                act.wait_ge(xs_norm, c + 1)
                blocks = slice(4 * c, 4 * c + 4)
                act.activation(xs_hi[:, blocks, :, :], xs[:, blocks, :, :], ACT.Copy).then_inc(xs_hi_out, 1)

            def wc_high(i):
                cols = slice(0, head_columns(i))
                act.wait_ge(wc_ready, i + 1)
                act.activation(wc_hi[:, i % WB, cols], wc[:, i % WB, cols], ACT.Copy).then_inc(wc_hi_out, 1)

            def convolved(i):
                act.wait_ge(conv_ps, i + 1)
                if i >= 8:
                    act.wait_ge(ct_ps, 4 * (i // 4 - 1))
                act.activation(cs[:, i % 8, :, :], B[i % 2][:].rearrange("p (b i) -> p b i", i=P),
                               ACT.Copy).then_inc(conv_out, 1)

            x_turned(0)
            for i in range(WB):
                wc_high(i)
            x_turned(1)
            deviation(0)
            x_turned(2)
            act.wait_ge(pads, 1)
            x_high(0)
            deviation(1)
            x_turned(3)
            x_high(1)
            deviation(2)
            x_high(2)
            convolved(0)
            wc_high(3)
            deviation(3)
            x_high(3)
            convolved(1)
            wc_high(4)
            for i in range(2, STEPS):
                if i < NBLK:
                    convolved(i)
                n = i - 5
                if 0 <= n < NT:
                    act.wait_ge(tok_ps, n + 1)
                    act.activation(tokens(n), B[4 + n % 2][:], ACT.Copy).then_inc(tok_out, 1)
                    act.wait_ge(tok_out, n + 1)
                    act.dma_start(acc_dram[P * col(n):P * col(n) + P, :], tokens(n)).then_inc(acc_st[n % NB], 16)
                    if n == 0:
                        act.dma_start(acc_dram[TOKENS:, :], tokens(0)).then_inc(spare_st, 16)
                    act.wait_ge(var_in, NG + n + 1)
                    act.activation(rstd_t[:], rstd_t[:], ACT.Sqrt).then_inc(sd_out, 1)
                n = i - 6
                if 0 <= n < NT:
                    act.wait_ge(xn_ready, n + 1)
                    act.dma_start(xn_dram[P * col(n):P * col(n) + P, :],
                                  xnb[:, n % XB, :, :].rearrange("p q i -> p (q i)")).then_inc(xn_st[n % XB], 16)
                    act.wait_ge(xnT_ps, n + 1)
                    if n >= 1:
                        act.wait_ge(logit_ps, n)
                    act.activation(xnT[:].rearrange("p q i -> p (q i)"), B[6][:], ACT.Copy).then_inc(xnT_out, 1)
                if 5 <= i + WB < NBLK:
                    wc_high(i + WB)
            for k in range(2):
                high_half(act, 0, k)

            act.wait_ge(ex_in, 1)
            act.activation(RT[1][:], RT[1][:], ACT.Exp).then_inc(ex_out, 1)
            for k in range(2, UNITS):
                high_half(act, 0, k)

            act.wait_ge(xg_ps, 1)
            act.activation(xT_hi[:], B[6][:].rearrange("p (q i) -> p q i", i=P), ACT.Copy).then_inc(xT_hi_out, 1)

            def act_tile(t, e):
                last = act.value_load(tile_last[0:1, bass.ds(t, 1)], min_val=0, max_val=1)

                def next_expert(*ks):
                    with act.If_ne(last.val, 0):
                        for k in ks:
                            act.wait_ge(unit_done, t * UNITS + (k + 1))
                            high_half(act, e + 1, k)

                def silu(j):
                    act.wait_ge(unit_done, t * UNITS + (2 * j + 1))
                    act.activation(h[:, j, :], B[2 * j][:], ACT.Silu).then_inc(silu_out, 1)

                def hi(j):
                    act.wait_ge(hT_ps, t * 2 + (j + 1))
                    act.activation(hT_hi[:, j, :, :], B[4 + j][:].rearrange("p (c n) -> p c n", n=P),
                                   ACT.Copy).then_inc(hT_hi_out, 1)

                silu(0)
                next_expert(0, 1)
                silu(1)
                hi(0)
                next_expert(2)
                act.wait_ge(xg_ps, t + 2)
                act.activation(xT_hi[:], B[6][:].rearrange("p (q i) -> p q i", i=P),
                               ACT.Copy).then_inc(xT_hi_out, 1)
                next_expert(3)
                hi(1)
                next_expert(4)
                act.wait_ge(unit_done, t * UNITS + UNITS)
                if not isinstance(t, int):
                    act.wait_ge(y_st, t * 16)
                act.activation(y[:].rearrange("p (q i) -> p q i", i=P), B[7][:].rearrange("p (i q) -> p q i", q=NQ), ACT.Copy, scale=slot_gate[:, bass.ds(t, 1)]).then_inc(y_out, 1)
                next_expert(5)

            act_tile(0, 0)
            with act.Fori(1, TILES) as t:
                live = act.value_load(tile_units[0:1, bass.ds(t, 1)], min_val=0, max_val=UNITS * E)
                with act.If_ne(live.val, 0):
                    act_tile(t, live // UNITS)
                    act.nop()

            for m in range(NT):
                b, g = m // NG, m % NG
                act.wait_ge(rows_ps, m + 1)
                if b >= 2:
                    act.wait_ge(out_st[b % 2], 16 * (b // 2))
                act.activation(ot[:, b % 2, :, P * g:P * g + P], B[m % 4][:].rearrange("p (q n) -> p q n", n=P),
                               ACT.Copy).then_inc(ot_out, 1)

        @block.tensor
        def _(pe):
            pe.wait_ge(consts, 1)
            pe.wait_ge(mix4_ready, 1)
            for j in range(NS):
                pe.transpose(B[5][:, D * j:D * j + D], mix4[:, j, :, :].rearrange("d q m -> d (q m)"), ident[0:D, 0:D])
            for q in range(NQ):
                ins = pe.transpose(B[5][:, P + E * q:P + E * q + E], gatew[:, q::NQ], ident[0:E, 0:E])
            ins.then_inc(small_ps, 1)
            pe.wait_ge(copies_ready, 1)
            pe.wait_ge(taps_in, 16 * NS)
            for n in range(NS):
                ins = pe.matmul(taps_view(n), copies[:].rearrange("d q m -> d (q m)"),
                                taps_nat[n][:].rearrange("m blk k -> m (blk k)"), start=True, stop=True)
            ins.then_inc(taps_ps, 1)

            def moments(c):
                for k in range(2):
                    pe.wait_ge(mom_ready, 2 * c + k + 1)
                    pe.matmul(B[6 + k][:, NBLK * c:NBLK * c + NBLK], same[:], mom[:, c % 2, (0, 4)[k], :],
                              start=True, stop=True).then_inc(mom_ps, 1)

            pe.wait_ge(pool_step, 6)

            def turn_x(c):
                for b in range(NB):
                    pe.wait_ge(x_blocks, NB * c + b + 1)
                    if c >= 1:
                        pe.wait_ge(xs_out, NB * (c - 1) + b + 1)
                    for k in range(4):
                        ins = pe.transpose(B[2 + b][:, P * k:P * k + P],
                                           X[:, b, 4 * c + k, :, :].rearrange("p q d -> p (q d)"), ident[:])
                    ins.then_inc(xt_ps0, 1)

            def conv(i):
                parts = [(blk, d) for n, blk, _ in head_parts(i) for d in range(LAGS[n] // NQ)]
                quarters = max(p[0] for p in parts) // 4 + 1
                pe.wait_ge(xs_lo_out, min(quarters, NG - 1))
                if quarters == NG:
                    pe.wait_ge(last_lo_out, 1)
                pe.wait_ge(wc_lo_out, i + 1)
                if i >= 2:
                    pe.wait_ge(conv_out, i - 1)
                out = B[i % 2][:].rearrange("p (b i) -> p b i", i=P)
                for a, (blk, d) in enumerate(parts):
                    cols, at = slice(P * a, P * a + P), slice(PAD - d, PAD - d + P)
                    pe.matmul(out, wc_hi[:, i % WB, cols], xs_hi[:, blk, :, at], start=(a == 0), stop=False)
                    pe.matmul(out, wc_hi[:, i % WB, cols], xs_lo[:, blk, :, at], start=False, stop=False)
                    ins = pe.matmul(out, wc_lo[:, i % WB, cols], xs_hi[:, blk, :, at],
                                    start=False, stop=(a == len(parts) - 1))
                ins.then_inc(conv_ps, 1)

            turn_x(0)
            turn_x(1)
            moments(0)
            turn_x(2)
            moments(1)
            turn_x(3)
            moments(2)
            conv(0)
            moments(3)
            conv(1)
            for i in range(2, STEPS):
                if i < NBLK:
                    conv(i)
                n = i - 4
                if 0 <= n < NT:
                    g, b = gb(n)
                    pe.wait_ge(conv_out, 4 * g + 4)
                    if n >= 2:
                        pe.wait_ge(resid, n - 1)
                    for k in range(4):
                        ins = pe.transpose(B[2 + n % 2][:, P * k:P * k + P], cs[:, (4 * g + k) % 8, b, :], ident[:])
                    ins.then_inc(ct_ps, 1)
                n = i - 5
                if 0 <= n < NT:
                    g, b = gb(n)
                    pe.wait_ge(resid, n + 1)
                    if n >= 2:
                        pe.wait_ge(tok_out, n - 1)
                    for q in range(NQ):
                        ins = pe.transpose(B[4 + n % 2][:, P * q:P * q + P], xc[:, n % 2, q, :], ident[:])
                    ins.then_inc(tok_ps, 1)
                n = i - 6
                if 0 <= n < NT:
                    pe.wait_ge(xn_ready, n + 1)
                    if n >= 1:
                        pe.wait_ge(xnT_out, n)
                    for q in range(NQ):
                        ins = pe.transpose(B[6][:, P * q:P * q + P], xnb[:, n % XB, q, :], ident[:])
                    ins.then_inc(xnT_ps, 1)
                n = i - 7
                if 0 <= n < NT:
                    pe.wait_ge(xnT_out, n + 1)
                    for q in range(NQ):
                        ins = pe.matmul(B[7][:, E * col(n):E * col(n) + E], xnT[:, q, :], gateT[:, q, :],
                                        start=(q == 0), stop=(q == NQ - 1))
                    ins.then_inc(logit_ps, 1)

            pe.wait_ge(mask_ready, 1)
            pe.wait_ge(consts, CONSTS)
            masks = RT[6][:].rearrange("p t e -> p (t e)")
            pe.matmul(B[0][:, 0:P], below[:], masks, start=True, stop=True)
            pe.matmul(B[1][:, 0:P], ones[:], masks, start=True, stop=True).then_inc(count_ps, 1)
            for a in range(2 * NT):
                pe.wait_ge(onehot, a + 1)
                ins = pe.matmul(B[2][:, 0:2 * SLOT_TILES], ohr[:, a % 2, :], oht[:, a, :, :].rearrange("p v t -> p (v t)"),
                                start=(a == 0), stop=(a == 2 * NT - 1))
                ins.then_inc(src_ps, 1)

            def turn_tokens(n):
                pe.wait_ge(xg_in, n * 16)
                for q in range(NQ):
                    ins = pe.transpose(B[6][:, P * q:P * q + P], xg[:, q, :], ident[:])
                ins.then_inc(xg_ps, 1)

            def product(bank, stat_hi, stat_lo, k, c, start, stop):
                hi, lo = w_hi[:, k, c, :], w_lo[:, k, c, :]
                pe.matmul(B[bank][:], stat_hi, hi, start=start, stop=False)
                pe.matmul(B[bank][:], stat_hi, lo, start=False, stop=False)
                return pe.matmul(B[bank][:], stat_lo, hi, start=False, stop=stop)

            def pe_tile(t, units):
                def up(k):
                    pe.wait_ge(lo_ready, units + k)
                    for c in range(4):
                        ins = product(k, xT_hi[:, c, :], xT_lo[:, c, :], k, c, c == 0, c == 3)
                    ins.then_inc(unit_done, 1)

                def turn_h(j):
                    pe.wait_ge(h_out, t * 2 + (j + 1))
                    for c in range(4):
                        ins = pe.transpose(B[4 + j][:, P * c:P * c + P], h[:, j, P * c:P * c + P], ident[:])
                    ins.then_inc(hT_ps, 1)

                def down(j, chunks):
                    for c in chunks:
                        ins = product(7, hT_hi[:, j, c, :], hT_lo[:, j, c, :], 4 + j, c,
                                      j == 0 and c == 0, j == 1 and c == 3)
                    return ins

                pe.wait_ge(xT_lo_out, t + 1)
                up(0)
                up(1)
                up(2)
                turn_h(0)
                up(3)
                turn_tokens(t + 2)
                pe.wait_ge(lo_ready, units + 4)
                pe.wait_ge(hT_lo_out, t * 2 + 1)
                if not isinstance(t, int):
                    pe.wait_ge(y_out, t)
                down(0, (0, 1))
                turn_h(1)
                down(0, (2, 3)).then_inc(unit_done, 1)
                pe.wait_ge(lo_ready, units + 5)
                pe.wait_ge(hT_lo_out, t * 2 + 2)
                down(1, range(4)).then_inc(unit_done, 1)

            turn_tokens(1)
            pe_tile(0, 1)
            with pe.Fori(1, TILES) as t:
                units = pe.value_load(tile_units[0:1, bass.ds(t, 1)], min_val=0, max_val=UNITS * E)
                with pe.If_ne(units.val, 0):
                    pe_tile(t, units)

            for m in range(NT):
                b, g = m // NG, m % NG
                pe.wait_ge(rows_in[b % 2], 16 * (b // 2 + 1))
                if m >= 4:
                    pe.wait_ge(ot_out, m - 3)
                for q in range(NQ):
                    ins = pe.transpose(B[m % 4][:, P * q:P * q + P], rows[:, b % 2, g, P * q:P * q + P], ident[:])
                ins.then_inc(rows_ps, 1)

        @block.vector
        def _(dve):
            steps = [0]

            def then_next(ins):
                steps[0] += 1
                ins.then_inc(dve_step, 1)
                dve.wait_ge(dve_step, steps[0])

            dve.wait_ge(consts, 1)
            dve.tensor_copy(copies[:], ident[0:D, 0:D].unsqueeze(1).broadcast_to([D, NQ, D])).then_inc(copies_ready, 1)
            dve.wait_ge(small_in, 32)
            dve.tensor_copy(mix4[:], mixw[:].rearrange("d (j m) -> d j m", j=NS).unsqueeze(2)
                            .broadcast_to([D, NS, NQ, D])).then_inc(mix4_ready, 1)
            dve.wait_ge(small_ps, 1)
            dve.tensor_copy(mixT[:], B[5][:, 0:NS * D].rearrange("p (j d) -> p j d", d=D)).then_inc(small_out, 1)
            dve.tensor_copy(gateT[:], B[5][:, P:P + NQ * E].rearrange("p (q e) -> p q e", e=E)).then_inc(small_out, 1)

            dve.wait_ge(taps_ps, 1)
            dve.wait_ge(taps_zeroed, NS)
            for n, k in enumerate(TAPS):
                for p in range(NQ):
                    at, rows_p = LAGS[n] - k - p, slice(D * p, D * p + D)
                    dve.tensor_copy(taps[n][rows_p, :, at:at + k],
                                    taps_view(n)[rows_p, :].rearrange("r (blk k) -> r blk k", k=k)).then_inc(taps_out, 1)

            def to_blocks(c):
                dve.wait_ge(x_in[c], 16 * NB)
                for b in range(NB):
                    dve.tensor_copy(X[:, b, 4 * c:4 * c + 4, :, :],
                                    xin[:, c % 2, b, :, :].rearrange("p q (k d) -> p k q d", d=D)
                                    ).then_inc(x_blocks, 1)

            def moment(c, k):
                return mom[:, c % 2, k, :]

            def row_moments(c):
                for b in range(NB):
                    dve.wait_ge(xs_out, NB * c + b + 1)
                    for k in range(4):
                        ins = dve.bn_stats(bn6[:, NB * k + b, :], xs[:, 4 * c + k, b, PAD:])
                then_next(ins)
                mean, dm, var = (moment(c, k) for k in range(3))
                dve.tensor_tensor(mean, bn6[:, :, 1], bn6[:, :, 4], ALU.add)
                then_next(dve.tensor_tensor(dm, bn6[:, :, 1], bn6[:, :, 4], ALU.subtract))
                dve.tensor_scalar(mean, mean, 0.5, None, ALU.mult).then_inc(mom_ready, 1)
                dve.tensor_tensor(var, bn6[:, :, 2], bn6[:, :, 5], ALU.add)
                then_next(dve.tensor_tensor(dm, dm, dm, ALU.mult))
                then_next(dve.scalar_tensor_tensor(out=var, in0=dm, scalar=P / 4.0, in1=var, op0=ALU.mult, op1=ALU.add))

            def second_moment(c):
                mean, var, dev, mean_all = (moment(c, k) for k in (0, 2, 3, 5))
                dve.wait_ge(mom_ps, 2 * c + 1)
                then_next(dve.tensor_copy(mean_all, B[6][:, NBLK * c:NBLK * c + NBLK]))
                then_next(dve.tensor_tensor(dev, mean, mean_all, ALU.subtract))
                then_next(dve.tensor_tensor(dev, dev, dev, ALU.mult))
                dve.scalar_tensor_tensor(out=moment(c, 4), in0=var, scalar=1.0 / P, in1=dev,
                                         op0=ALU.mult, op1=ALU.add).then_inc(mom_ready, 1)

            def variance(c):
                dve.wait_ge(mom_ps, 2 * c + 2)
                dve.tensor_scalar(moment(c, 3), B[7][:, NBLK * c:NBLK * c + NBLK], EPS_C, None,
                                  ALU.add).then_inc(var_in, 1)

            def normalise(c):
                dev, mean_all = moment(c, 3), moment(c, 5)
                dve.wait_ge(sd_out, c + 1)
                then_next(dve.reciprocal(dev, dev))
                for k in range(4):
                    for b in range(NB):
                        m, v = NB * k + b, xs[:, 4 * c + k, b, PAD:]
                        ins = dve.tensor_scalar(v, v, mean_all[:, m:m + 1], dev[:, m:m + 1], ALU.subtract, ALU.mult)
                ins.then_inc(xs_norm, 1)

            to_blocks(0)
            to_blocks(1)
            row_moments(0)
            for c in range(NG):
                second_moment(c)
                if c + 2 < NG:
                    to_blocks(c + 2)
                variance(c)
                if c + 1 < NG:
                    row_moments(c + 1)
                normalise(c)
            x_low(dve, NG - 1)

            for i in range(EARLY - WB, STEPS):
                n = i - 4
                if 0 <= n < NT:
                    g, b = gb(n)
                    dve.wait_ge(ct_ps, n + 1)
                    if n >= 2:
                        dve.wait_ge(tok_ps, n - 1)
                    dve.tensor_tensor(xc[:, n % 2, :, :].rearrange("p q (k d) -> p k q d", d=D),
                                      B[2 + n % 2][:].rearrange("p (k q d) -> p k q d", q=NQ, d=D),
                                      X[:, b, 4 * g:4 * g + 4, :, :], ALU.add).then_inc(resid, 1)
                n = i - 5
                if 0 <= n < NT:
                    dve.wait_ge(tok_out, n + 1)
                    then_next(dve.bn_stats(st6[:], tokens(n)))
                    then_next(dve.bn_aggr(mv[:], st6[:]))
                    dve.tensor_scalar(rstd_t[:], mv[:, 1:2], EPS_T, None, ALU.add).then_inc(var_in, 1)
                    dve.wait_ge(sd_out, NG + n + 1)
                    then_next(dve.reciprocal(rstd_t[:], rstd_t[:]))
                    if n >= XB:
                        dve.wait_ge(xn_st[n % XB], 16 * (n // XB))
                        dve.wait_ge(xnT_ps, n + 1 - XB)
                    dve.tensor_scalar(xnb[:, n % XB, :, :].rearrange("p q i -> p (q i)"), tokens(n), mv[:, 0:1], rstd_t[:],
                                      ALU.subtract, ALU.mult).then_inc(xn_ready, 1)
                if EARLY <= i + WB < NBLK:
                    wc_low(dve, i + WB)

            lg, ex, p, m1, m2, rest, both, before, base, sel = (RT[k][:] for k in range(10))
            scan = (RT[10][:], RT[11][:])

            def wide(v):
                return v.unsqueeze(2).broadcast_to([P, NT, E])

            ranks = rank8[:].unsqueeze(1).broadcast_to([P, NT, E])
            top, total, rsum, p1, p2, psum2, pick = (small[:, k, :] for k in range(7))
            cnt, ntile, end = (small[:, 7 + k, 0:E] for k in range(3))
            start_t = small[:, 7, E:2 * E]

            dve.wait_ge(logit_ps, NT)
            for b in range(2):
                dve.wait_ge(acc_st[b], 16 * NG)
            dve.wait_ge(consts, CONSTS)
            then_next(dve.tensor_copy(lg, B[7][:, 0:NT * E].rearrange("p (t e) -> p t e", e=E)))
            then_next(dve.tensor_reduce(top, lg, AX_X, ALU.max))
            dve.tensor_tensor(ex, lg, wide(top), ALU.subtract).then_inc(ex_in, 1)

            def pick_first(values, biggest, mask):
                then_next(dve.tensor_tensor(sel, values, wide(biggest), ALU.is_equal))
                then_next(dve.tensor_tensor(sel, sel, ranks, ALU.mult))
                then_next(dve.tensor_reduce(pick, sel, AX_X, ALU.max))
                then_next(dve.tensor_tensor(mask, ranks, wide(pick), ALU.is_equal))

            pick_first(lg, top, m1)
            then_next(dve.scalar_tensor_tensor(out=rest, in0=m1, scalar=-3.0e38, in1=lg, op0=ALU.mult, op1=ALU.add))
            then_next(dve.tensor_reduce(top, rest, AX_X, ALU.max))
            pick_first(rest, top, m2)
            dve.tensor_tensor(both, m1, m2, ALU.add).then_inc(mask_ready, 1)

            dve.wait_ge(ex_out, 1)
            then_next(dve.tensor_reduce(total, ex, AX_X, ALU.add))
            then_next(dve.reciprocal(rsum, total))
            then_next(dve.tensor_tensor(p, ex, wide(rsum), ALU.mult))
            for mask, pk in ((m1, p1), (m2, p2)):
                then_next(dve.tensor_tensor(sel, p, mask, ALU.mult))
                then_next(dve.tensor_reduce(pk, sel, AX_X, ALU.add))
            then_next(dve.tensor_tensor(psum2, p1, p2, ALU.add))
            then_next(dve.reciprocal(psum2, psum2))
            dve.tensor_tensor(gates[:, 0, :], p1, psum2, ALU.mult)
            then_next(dve.tensor_tensor(gates[:, 1, :], p2, psum2, ALU.mult))

            dve.wait_ge(count_ps, 1)
            whole = B[1][:, 0:NT * E].rearrange("p (t e) -> p t e", e=E)
            dve.memset(scan[0][:, 0:1, :], 0.0)
            then_next(dve.tensor_copy(scan[0][:, 1:, :], whole[:, 0:NT - 1, :]))
            a = 0
            for sft in (1, 2, 4, 8):
                dve.tensor_copy(scan[1 - a][:, 0:sft, :], scan[a][:, 0:sft, :])
                then_next(dve.tensor_tensor(scan[1 - a][:, sft:, :], scan[a][:, sft:, :],
                                            scan[a][:, 0:NT - sft, :], ALU.add))
                a = 1 - a
            then_next(dve.tensor_tensor(cnt, scan[a][:, NT - 1, :], whole[:, NT - 1, :], ALU.add))
            over = cmp[:, 0:E * 16].rearrange("p (e k) -> p e k", k=16)
            then_next(dve.tensor_tensor(over, cnt.unsqueeze(2).broadcast_to([P, E, 16]),
                                        thresholds[:].unsqueeze(1).broadcast_to([P, E, 16]), ALU.is_gt))
            then_next(dve.tensor_reduce(ntile, over, AX_X, ALU.add))
            then_next(dve.tensor_scalar(ntile, ntile, 1.0, None, ALU.max))
            then_next(dve.tensor_copy(end, ntile))
            for e in range(1, E):
                then_next(dve.tensor_tensor(end[:, e:e + 1], end[:, e:e + 1], end[:, e - 1:e], ALU.add))
            then_next(dve.tensor_tensor(start_t, end, ntile, ALU.subtract))
            then_next(dve.tensor_tensor(before, B[0][:, 0:NT * E].rearrange("p (t e) -> p t e", e=E), scan[a], ALU.add))
            then_next(dve.scalar_tensor_tensor(out=base, in0=start_t.unsqueeze(1).broadcast_to([P, NT, E]),
                                               scalar=float(P), in1=before, op0=ALU.mult, op1=ALU.add))
            for j, mask in enumerate((m1, m2)):
                then_next(dve.tensor_tensor(sel, base, mask, ALU.mult))
                then_next(dve.tensor_reduce(p1, sel, AX_X, ALU.add))
                then_next(dve.tensor_copy(sl_i[:, 1, NT * j:NT * j + NT], p1))
            then_next(dve.tensor_scalar(sl_i[:, 0, :], sl_i[:, 1, :], 7, None, ALU.arith_shift_right))
            then_next(dve.tensor_copy(sl_f[:, 0, :], sl_i[:, 0, :]))
            then_next(dve.tensor_scalar(sl_i[:, 0, :], sl_i[:, 1, :], P - 1, None, ALU.bitwise_and))
            then_next(dve.tensor_copy(sl_f[:, 1, :], sl_i[:, 0, :]))
            for b in range(2, NB):
                dve.wait_ge(acc_st[b], 16 * NG)
            hot, weighted = oht[:, :, 0, :], oht[:, :, 1, :]
            then_next(dve.tensor_tensor(hot, iota[:, 0:SLOT_TILES].unsqueeze(1).broadcast_to([P, 2 * NT, SLOT_TILES]),
                                        sl_f[:, 0, :].unsqueeze(2).broadcast_to([P, 2 * NT, SLOT_TILES]), ALU.is_equal))
            then_next(dve.tensor_tensor(weighted, hot, gates[:].rearrange("p j t -> p (j t)").unsqueeze(2)
                                        .broadcast_to([P, 2 * NT, SLOT_TILES]), ALU.mult))
            for j in range(2):
                ins = dve.tensor_tensor(hot[:, NT * j:NT * j + NT, :], hot[:, NT * j:NT * j + NT, :],
                                        tokid[:].unsqueeze(2).broadcast_to([P, NT, SLOT_TILES]), ALU.mult)
            then_next(ins)
            for a in range(2 * NT):
                if a >= 2:
                    dve.wait_ge(src_ps, a - 1)
                dve.tensor_scalar(ohr[:, a % 2, :], iota[:], sl_f[:, 1, a:a + 1], None,
                                  ALU.is_equal).then_inc(onehot, 1)
            passed = cmp[0:1, :].rearrange("p (t e) -> p t e", e=E)
            then_next(dve.tensor_tensor(passed, iota[0:1, 0:SLOT_TILES].unsqueeze(2).broadcast_to([1, SLOT_TILES, E]),
                                        end[0:1, :].unsqueeze(1).broadcast_to([1, SLOT_TILES, E]), ALU.is_ge))
            te = sl_f[0:1, :, :].rearrange("p a n -> p (a n)")[:, 0:SLOT_TILES]
            then_next(dve.tensor_reduce(te, passed, AX_X, ALU.add))
            flag, units = cmp[0:1, 0:TILES], cmp[0:1, P:P + TILES]
            dve.tensor_scalar(flag, te[:, 0:TILES], float(E), None, ALU.is_lt)
            then_next(dve.tensor_scalar(units, te[:, 0:TILES], float(UNITS), 1.0, ALU.mult, ALU.add))
            dve.tensor_tensor(tile_units[:], units, flag, ALU.mult)
            then_next(dve.tensor_scalar(te, te, float(E - 1), None, ALU.min))
            dve.tensor_tensor(tile_last[:], te[:, 1:], te[:, 0:TILES], ALU.subtract).then_inc(routed, 1)
            dve.wait_ge(src_ps, 2 * NT)
            number, empty = cmp[:, 0:SLOT_TILES], cmp[:, P:P + SLOT_TILES]
            dve.tensor_copy(slot_gate[:], B[2][:, SLOT_TILES:2 * SLOT_TILES])
            then_next(dve.tensor_copy(number, B[2][:, 0:SLOT_TILES]))
            dve.tensor_scalar(src_i[:], number, 1.0, 0.0, ALU.subtract, ALU.max)
            then_next(dve.tensor_scalar(empty, number, 0.0, None, ALU.is_equal))
            then_next(dve.tensor_tensor(empty, empty, spare[:], ALU.mult))
            dve.scalar_tensor_tensor(out=dst_i[:], in0=number, scalar=-1.0, in1=empty,
                                     op0=ALU.add, op1=ALU.add).then_inc(routed, 1)

            def xT_rest(n):
                dve.wait_ge(xT_hi_out, n)
                dve.tensor_tensor(xT_lo[:], B[6][:].rearrange("p (q i) -> p q i", i=P), xT_hi[:],
                                  ALU.subtract).then_inc(xT_lo_out, 1)

            def dve_tile(t, e):
                last = dve.value_load(tile_last[0:1, bass.ds(t, 1)], min_val=0, max_val=1)

                def next_expert(*ks):
                    with dve.If_ne(last.val, 0):
                        for k in ks:
                            low_half(dve, e + 1, k)

                def gate_up(j):
                    dve.wait_ge(silu_out, t * 2 + (j + 1))
                    dve.wait_ge(unit_done, t * UNITS + (2 * j + 2))
                    dve.tensor_tensor(h[:, j, :], B[2 * j + 1][:], h[:, j, :], ALU.mult).then_inc(h_out, 1)

                def rest_of_hT(j):
                    dve.wait_ge(hT_hi_out, t * 2 + (j + 1))
                    dve.tensor_tensor(hT_lo[:, j, :, :], B[4 + j][:].rearrange("p (c n) -> p c n", n=P),
                                      hT_hi[:, j, :, :], ALU.subtract).then_inc(hT_lo_out, 1)

                gate_up(0)
                next_expert(0, 1)
                rest_of_hT(0)
                gate_up(1)
                next_expert(2)
                xT_rest(t + 2)
                next_expert(3)
                rest_of_hT(1)
                next_expert(4, 5)

            xT_rest(1)
            if POOL_UNITS < UNITS:
                dve.wait_ge(lo_ready, POOL_UNITS)
            for k in range(POOL_UNITS, UNITS):
                low_half(dve, 0, k)
            dve_tile(0, 0)
            with dve.Fori(1, TILES) as t:
                live = dve.value_load(tile_units[0:1, bass.ds(t, 1)], min_val=0, max_val=UNITS * E)
                with dve.If_ne(live.val, 0):
                    dve_tile(t, live // UNITS)
                    dve.nop()


_INS = ["x", "L0_conv_w3", "L0_conv_w7", "L0_conv_w15", "L0_conv_w_mix", "L0_ffn_gate_w",
        "L0_ffn_w1", "L0_ffn_w2", "L0_ffn_w3"]


def kernel(**inputs):
    import numpy as _np
    import concourse.bacc as _bacc
    from concourse import mybir as _mybir
    from concourse.bass_utils import run_bass_kernel_spmd as _run

    nc = _bacc.Bacc("TRN2", target_bir_lowering=False, num_devices=1)
    arrays, args = {}, []
    for name in _INS:
        a = _np.ascontiguousarray(inputs[name])
        arrays[f"in_{name}"] = a
        args.append(nc.dram_tensor(f"in_{name}", a.shape, _mybir.dt.from_np(a.dtype), kind="ExternalInput").ap())
    args.append(nc.dram_tensor("out_x", inputs["x"].shape, F32, kind="ExternalOutput").ap())
    metaformer(nc, *args)
    r = _run(nc, [arrays], core_ids=[0])
    return r.results[0]["out_x"]
```

```python
from contextlib import ExitStack

import concourse.bass as bass
from concourse import mybir

F32 = mybir.dt.float32
F32R = mybir.dt.float32r
I32 = mybir.dt.int32
ALU = mybir.AluOpType
ACT = mybir.ActivationFunctionType
AX_X = mybir.AxisListType.X

P = 128
NB = 4
L = 512
C = 512
NQ = L // P
D = 32
NBLK = C // D
TAPS = (3, 7, 15)
NS = len(TAPS)
LAGS = tuple(NQ * -(-(k + NQ - 1) // NQ) for k in TAPS)
PAD = max(LAGS) // NQ - 1
CHUNKS = NS * max(LAGS) // NQ
WB = 3
XB = 4
NG = C // P
NT = NB * NG
E = 8
TILES = NT * 2 + E - 1
SLOT_TILES = 2 * -(-(TILES + 2) // 2)
POOL_UNITS = 4
UNITS = 6
TOKENS = NT * P
EPS_C = 1e-6
EPS_T = 1e-5


def metaformer(nc, x, w3c, w7c, w15c, w_mix, gate_w, w1, w2, w3, out):
    taps_dram = (w3c, w7c, w15c)
    x_nat = x.rearrange("b (i q) h w -> b i q (h w)", q=NQ)
    out_nat = out.rearrange("b (i q) h w -> b i q (h w)", q=NQ)

    def raw_src(e, k):
        if k < 4:
            w = (w1, w3)[k % 2]
            cols = slice(512 * (k // 2), 512 * (k // 2) + 512)
            return w[bass.ds(e, 1), :, cols].rearrange("e (i q) n -> i (e q) n", q=NQ)
        rows = slice(512 * (k - 4), 512 * (k - 4) + 512)
        return w2[bass.ds(e, 1), rows, :].rearrange("e (c p) n -> p (e c) n", p=P)

    with ExitStack() as ctx:
        def sb(name, shape, dt=F32, c=ctx):
            return c.enter_context(nc.sbuf_tensor(name, shape, dt))

        def sem(name):
            return ctx.enter_context(nc.semaphore(name))

        xn_dram = nc.dram_tensor("xn_rows", [TOKENS, L], F32, kind="Internal").ap()
        acc_dram = nc.dram_tensor("acc_rows", [TOKENS + P, L], F32, kind="Internal").ap()

        ident = sb("ident", [P, P])
        below = sb("below", [P, P])
        ones = sb("ones", [P, P])
        iota = sb("iota", [P, P])
        thresholds = sb("thresholds", [P, 16])
        rank8 = sb("rank8", [P, E])
        earlier = sb("earlier", [P, E, E])
        tokid = sb("tokid", [P, NT])
        spare = sb("spare", [P, SLOT_TILES])
        src_i = sb("src_i", [P, SLOT_TILES], I32)
        dst_i = sb("dst_i", [P, SLOT_TILES], I32)
        slot_gate = sb("slot_gate", [P, SLOT_TILES])
        gather_at = sb("gather_at", [P, 1], I32)
        add_at = sb("add_at", [P, 1], I32)
        tile_expert = sb("tile_expert", [1, TILES], I32)
        tiles_before = sb("tiles_before", [1, 1], I32)
        last_at = sb("last_at", [P, NT])
        tile_last = sb("tile_last", [1, TILES], I32)

        with ExitStack() as s:
            X = sb("X", [P, NB, NBLK, NQ, D], c=s)
        with ExitStack() as s:
            ex = sb("ex", [P, NT, E], c=s)
            base = sb("base", [P, NT, E], c=s)
            picked = sb("picked", [P, 2, NT, E], c=s)
            small = sb("small", [P, 6, 2 * NT], c=s)
            over = sb("over", [P, E, 16], c=s)
            ntile, end, start_t = (sb(n, [P, E], c=s) for n in ("ntile", "end", "start_t"))
            upto = sb("upto", [P, E, E], c=s)
            passed = sb("passed", [1, SLOT_TILES, E], c=s)
            te = sb("te", [1, 3, SLOT_TILES], c=s)
            number, empty, final, last_number = (sb(n, [P, SLOT_TILES], c=s)
                                                 for n in ("number", "empty", "final", "last_number"))
            last_token = sb("last_token", [P, 2], c=s)
            sl_i = sb("sl_i", [P, 3, 2 * NT], I32, c=s)
            sl_f = sb("sl_f", [P, 2, 2 * NT], c=s)
            gate_hi = sb("gate_hi", [P, 2 * NT], F32R, c=s)
            gate_lo = sb("gate_lo", [P, 2 * NT], c=s)
            hot = sb("hot", [P, 2 * NT, SLOT_TILES], c=s)
            hot_token = sb("hot_token", [P, 2 * NT, SLOT_TILES], F32R, c=s)
            hot_gate = sb("hot_gate", [P, 2 * NT, 2, SLOT_TILES], F32R, c=s)
        with ExitStack() as s:
            ot = sb("ot", [P, NB, NQ, C], c=s)
        sb("held1", [P, NB * NBLK * P])
        with ExitStack() as s:
            xc = sb("xc", [P, 2, NQ, P], c=s)
            xnT = sb("xnT", [P, 2, NQ, P], c=s)
            xs = sb("xs", [P, NBLK, NB, PAD + P], c=s)
            xs_hi = sb("xs_hi", [P, NBLK, NB, PAD + P], F32R, c=s)
            wc = sb("wc", [P, WB, CHUNKS * P], c=s)
            wc_hi = sb("wc_hi", [P, WB, CHUNKS * P], F32R, c=s)
            taps = [sb(f"taps{n}", [P, NBLK, v], c=s) for n, v in enumerate(LAGS)]
            mixT = sb("mixT", [P, NS, D], c=s)
            xin = sb("xin", [P, 2, NB, NQ, P], c=s)
            same = sb("same", [P, P], c=s)
        with ExitStack() as s:
            taps_nat = [sb(f"taps_nat{n}", [D, NBLK, k], c=s) for n, k in enumerate(TAPS)]
            copies = sb("copies", [D, NQ, D], c=s)
            mixw = sb("mixw", [D, NS * D], c=s)
            gatew = sb("gatew", [E, L], c=s)
            mix4 = sb("mix4", [D, NS, NQ, D], c=s)
        with ExitStack() as s:
            sb("held_xc", [P, 4 * NQ * P], c=s)
            xs_lo = sb("xs_lo", [P, NBLK, NB, PAD + P], F32R, c=s)
            sb("held_xs_hi", [P, NBLK, NB, PAD + P], c=s)
            wc_lo = sb("wc_lo", [P, WB, CHUNKS * P], F32R, c=s)
        with ExitStack() as s:
            w_lo = sb("w_lo", [P, UNITS, 4, 512], F32R, c=s)
            w_hi = sb("w_hi", [P, UNITS, 4, 512], F32R, c=s)
            w_raw = sb("w_raw", [P, UNITS, 4, 512], c=s)
        with ExitStack() as s:
            sb("held_halves", [P, 2 * UNITS * 4 * 512], c=s)
            rows = sb("rows", [P, NB, NG, L], c=s)
            last_hot = sb("last_hot", [P, NT * P], F32R, c=s)
        sb("held2", [P, 3 * UNITS * 4 * 512])
        with ExitStack() as s:
            cs = sb("cs", [P, 8, NB, P], c=s)
            xnb = sb("xnb", [P, XB, NQ, P], c=s)
            masks = sb("masks", [P, 2, NT, E], c=s)
            running = sb("running", [P, NT + 1, E], c=s)
            logits = sb("logits", [P, NT, E], c=s)
            counts = sb("counts", [P, 2, NT, E], c=s)
            top1 = sb("top1", [P, NT], c=s)
            rest, sel = (sb(n, [P, NT // 2, E], c=s) for n in ("rest", "sel"))
            top2, pick = (sb(n, [P, NT // 2], c=s) for n in ("top2", "pick"))
        with ExitStack() as s:
            sb("held_cs", [P, (NB * 8 + XB * NQ) * P], c=s)
            bn6 = sb("bn6", [P, NBLK, 6], c=s)
            mom = sb("mom", [P, 2, 6, NBLK], c=s)
        with ExitStack() as s:
            row_hot = sb("row_hot", [P, 2 * NT, P], F32R, c=s)
        with ExitStack() as s:
            hT_hi = sb("hT_hi", [P, 2, 4, P], F32R, c=s)
            hT_lo = sb("hT_lo", [P, 2, 4, P], F32R, c=s)
            y = sb("y", [P, L], c=s)
            y_hi = sb("y_hi", [P, NQ, P], F32R, c=s)
            y_lo = sb("y_lo", [P, NQ, P], F32R, c=s)
            sb("held_row_hot", [P, 512], c=s)
            xg = sb("xg", [P, NQ, P], c=s)
            xT_hi = sb("xT_hi", [P, NQ, P], F32R, c=s)
            xT_lo = sb("xT_lo", [P, NQ, P], F32R, c=s)
            h = sb("h", [P, 2, 512], c=s)
        sb("held3", [P, 7104])
        gateT = sb("gateT", [P, NQ, E])
        st6 = sb("st6", [P, 6])
        mv = sb("mv", [P, 2])
        rstd_t = sb("rstd_t", [P, 1])

        B = [ctx.enter_context(nc.psum_tensor(f"bank{n}", [P, 512], F32)) for n in range(8)]

        x_in = [sem(f"x_in{c}") for c in range(NG)]
        x_blocks = [sem(f"x_blocks{c}") for c in range(NG)]
        taps_in, small_in = sem("taps_in"), sem("small_in")
        copies_ready, taps_ps, taps_out = sem("copies_ready"), sem("taps_ps"), sem("taps_out")
        taps_zeroed, consts = sem("taps_zeroed"), sem("consts")
        pool_step, dve_step = sem("pool_step"), sem("dve_step")
        mix4_ready, small_ps, small_out = sem("mix4_ready"), sem("small_ps"), sem("small_out")
        xt_ps0, xs_out, pads = sem("xt_ps0"), sem("xs_out"), sem("pads")
        mom_ready, mom_ps = sem("mom_ready"), sem("mom_ps")
        var_in, sd_out = sem("var_in"), sem("sd_out")
        xs_norm, xs_hi_out, xs_lo_out = sem("xs_norm"), sem("xs_hi_out"), sem("xs_lo_out")
        last_lo_out = sem("last_lo_out")
        wc_ready, wc_hi_out, wc_lo_out = sem("wc_ready"), sem("wc_hi_out"), sem("wc_lo_out")
        conv_ps, conv_out = sem("conv_ps"), sem("conv_out")
        ct_ps, resid = sem("ct_ps"), sem("resid")
        tok_ps, tok_out, xn_ready = sem("tok_ps"), sem("tok_out"), sem("xn_ready")
        xn_st = [sem(f"xn_st{n}") for n in range(XB)]
        acc_st = [sem(f"acc_st{b}") for b in range(NB)]
        spare_st = sem("spare_st")
        gather_index, add_index = sem("gather_index"), sem("add_index")
        xnT_ps, xnT_out, logit_ps = sem("xnT_ps"), sem("xnT_out"), sem("logit_ps")
        ex_in, ex_out = sem("ex_in"), sem("ex_out")
        mask_ready, count_ps, count_out, lg_out = (sem("mask_ready"), sem("count_ps"), sem("count_out"),
                                                   sem("lg_out"))
        rows_hot, slot_ps, gates_hot, gate_ps = sem("rows_hot"), sem("slot_ps"), sem("gates_hot"), sem("gate_ps")
        src_ready, tables_ready, gate_ready = sem("src_ready"), sem("tables_ready"), sem("gate_ready")
        raw_in = [sem(f"raw_in{k}") for k in range(UNITS)]
        hi_ready = [sem(f"hi_ready{k}") for k in range(UNITS)]
        lo_ready = [sem(f"lo_ready{k}") for k in range(UNITS)]
        xg_in, xg_ps, xT_hi_out, xT_lo_out = sem("xg_in"), sem("xg_ps"), sem("xT_hi_out"), sem("xT_lo_out")
        unit_done = sem("unit_done")
        silu_out, h_out, hT_ps, hT_hi_out, hT_lo_out = (sem("silu_out"), sem("h_out"), sem("hT_ps"),
                                                        sem("hT_hi_out"), sem("hT_lo_out"))
        y_out, y_st = sem("y_out"), sem("y_st")
        all_added = sem("all_added")
        rows_in = [sem(f"rows_in{b}") for b in range(NB)]
        y_hi_out, y_lo_out, last_hot_ready = sem("y_hi_out"), sem("y_lo_out"), sem("last_hot_ready")
        rows_ps, out_st = sem("rows_ps"), sem("out_st")
        ot_out = [sem("ot_out_act"), sem("ot_out_dve")]

        CONSTS = 8

        STEPS = NBLK + 7

        BATCHES = ((0, 4), (4, 8), (8, NT))

        def counted_at(i):
            return {BATCHES[g][1] + 7: g for g in range(len(BATCHES) - 1)}.get(i)

        def gb(n):
            return n // NB, n % NB

        def tokens(n):
            g, b = gb(n)
            return X[:, b, 4 * g:4 * g + 4, :, :].rearrange("p k q d -> p (k q d)")

        def col(n):
            g, b = gb(n)
            return NG * b + g

        def high_half(eng, e, k):
            eng.wait_ge(raw_in[k], (e + 1) * 16)
            eng.activation(w_hi[:, k, :, :], w_raw[:, UNITS - 1 - k, :, :], ACT.Copy).then_inc(hi_ready[k], 1)

        def low_half(eng, e, k):
            eng.wait_ge(hi_ready[k], e + 1)
            eng.tensor_tensor(w_lo[:, k, :, :], w_raw[:, UNITS - 1 - k, :, :], w_hi[:, k, :, :],
                              ALU.subtract).then_inc(lo_ready[k], 1)

        def taps_view(n):
            at = NBLK * sum(TAPS[:n])
            return B[0][:, at:at + NBLK * TAPS[n]]

        def head_parts(i):
            return [(*divmod(NS * i + j, NBLK), j) for j in range(NS)]

        def head_columns(i):
            return sum(LAGS[n] * D for n, _, _ in head_parts(i))

        def wc_low(eng, i):
            cols = slice(0, head_columns(i))
            eng.wait_ge(wc_hi_out, i + 1)
            eng.tensor_tensor(wc_lo[:, i % WB, cols], wc[:, i % WB, cols], wc_hi[:, i % WB, cols],
                              ALU.subtract).then_inc(wc_lo_out, 1)

        def to_blocks(eng, copy, c):
            eng.wait_ge(x_in[c], 16 * NB)
            for b in range(NB):
                copy(X[:, b, 4 * c:4 * c + 4, :, :],
                     xin[:, c % 2, b, :, :].rearrange("p q (k d) -> p k q d", d=D)).then_inc(x_blocks[c], 1)

        def x_low(eng, c):
            eng.wait_ge(xs_hi_out, c + 1)
            blocks = slice(4 * c, 4 * c + 4)
            eng.tensor_tensor(xs_lo[:, blocks, :, :], xs[:, blocks, :, :], xs_hi[:, blocks, :, :],
                              ALU.subtract).then_inc(xs_lo_out if c < NG - 1 else last_lo_out, 1)

        OB = 6
        EARLY = 5

        block = ctx.enter_context(nc.Block())

        @block.sync
        def _(sp):
            for c in range(NG):
                if c >= 2:
                    sp.wait_ge(x_blocks[c - 2], NB)
                for b in range(NB):
                    sp.dma_start(xin[:, c % 2, b, :, :], x_nat[b][:, :, P * c:P * c + P]).then_inc(x_in[c], 16)

            def load_unit(e, k):
                sp.dma_start(w_raw[:, UNITS - 1 - k, :, :], raw_src(e, k)).then_inc(raw_in[k], 16)

            for c in range(2, NG):
                sp.wait_ge(x_blocks[c], NB)
            sp.wait_ge(mom_ps, 2 * NG)
            for k in range(UNITS):
                if k == 2:
                    sp.wait_ge(xnT_ps, NT)
                load_unit(0, k)
            with sp.Fori(1, E) as e:
                for k in range(UNITS):
                    sp.wait_ge(lo_ready[k], e)
                    load_unit(e, k)

            sp.wait_ge(tables_ready, 1)
            before = sp.value_load(tiles_before[0:1, 0:1], min_val=E - 1, max_val=TILES - 1)
            for k in range(UNITS):
                sp.wait_ge(lo_ready[k], E)
            sp.wait_ge(y_st, before * 16)
            for b in range(NB):
                sp.dma_start(rows[:, b, :, :], acc_dram[C * b:C * b + C, :].rearrange("(g p) l -> p g l", p=P)
                             ).then_inc(rows_in[b], 16)
            for m in range(NB * 2):
                for part in ot_out:
                    sp.wait_ge(part, m + 1)
                b, q = m // 2, 2 * (m % 2)
                sp.dma_start(out_nat[b][:, q:q + 2, :], ot[:, b, q:q + 2, :]).then_inc(out_st, 16)
            sp.wait_ge(out_st, 16 * NB * 2)
            sp.wait_ge(all_added, 1)

        @block.gpsimd
        def _(pool):
            steps = [0]

            def then_next(ins):
                steps[0] += 1
                ins.then_inc(pool_step, 1)
                pool.wait_ge(pool_step, steps[0])

            for n in range(NS):
                pool.memset(taps[n][:], 0.0).then_inc(taps_zeroed, 1)
            pool.memset(xs[:, :, :, 0:PAD], 0.0).then_inc(pads, 1)
            then_next(pool.memset(ident[:], 0.0))
            pool.affine_select(out=ident[:], in_=ident[:], compare_op=ALU.not_equal, fill=1.0, base=0,
                               pattern=[[-1, P]], channel_multiplier=1).then_inc(consts, 1)
            then_next(pool.memset(same[:], 0.0))
            for a in range(NQ):
                v = same[:].rearrange("p (q m) -> p q m", q=NQ)
                then_next(pool.affine_select(out=v, in_=v, compare_op=ALU.not_equal, fill=1.0 / NQ,
                                             base=-D * a, pattern=[[0, NQ], [-1, D]], channel_multiplier=1))
            pool.memset(ones[:], 1.0).then_inc(consts, 1)
            pool.wait_ge(consts, 2)
            pool.affine_select(out=below[:], in_=ones[:], compare_op=ALU.is_gt, fill=0.0, base=0,
                               pattern=[[1, P]], channel_multiplier=-1).then_inc(consts, 1)

            flat = dict(allow_small_or_imprecise_dtypes=True)
            pool.iota(iota[:], pattern=[[1, P]], base=0, channel_multiplier=0, **flat).then_inc(consts, 1)
            pool.iota(thresholds[:], pattern=[[P, 16]], base=0, channel_multiplier=0, **flat).then_inc(consts, 1)
            pool.iota(rank8[:], pattern=[[-1, E]], base=E, channel_multiplier=0, **flat).then_inc(consts, 1)
            pool.iota(spare[:], pattern=[[0, SLOT_TILES]], base=TOKENS + 1, channel_multiplier=1,
                      **flat).then_inc(consts, 1)
            pool.iota(tokid[:], pattern=[[P, NG], [C, NB]], base=1, channel_multiplier=1, **flat).then_inc(consts, 1)

            def multiply_taps(i):
                if i >= WB:
                    pool.wait_ge(conv_ps, i - WB + 1)
                parts, at = head_parts(i), 0
                for n in sorted({p[0] for p in parts}):
                    run = [p for p in parts if p[0] == n]
                    nb, v, blk, j = len(run), LAGS[n], run[0][1], run[0][2]
                    ins = pool.tensor_tensor(
                        wc[:, i % WB, at:at + nb * v * D].rearrange("p (b v d) -> p b v d", b=nb, v=v),
                        taps[n][:, blk:blk + nb, ::-1].unsqueeze(3).broadcast_to([P, nb, v, D]),
                        mixT[:, j:j + nb, :].unsqueeze(2).broadcast_to([P, nb, v, D]), ALU.mult)
                    at += nb * v * D
                ins.then_inc(wc_ready, 1)

            pool.wait_ge(taps_out, NS * NQ)
            pool.wait_ge(small_out, 2)
            for i in range(WB):
                multiply_taps(i)
            for i in range(WB):
                wc_low(pool, i)
            x_low(pool, 0)
            x_low(pool, 1)
            multiply_taps(WB)
            x_low(pool, 2)
            wc_low(pool, WB)
            multiply_taps(WB + 1)
            wc_low(pool, WB + 1)
            for i in range(EARLY, NBLK):
                multiply_taps(i)
            pool.wait_ge(logit_ps, NT)
            for k in range(POOL_UNITS):
                low_half(pool, 0, k)

            def gather(index):
                pool.indirect_dma_start(
                    out=xg[:].rearrange("p q i -> p (q i)"), out_offset=None, in_=xn_dram,
                    in_offset=bass.IndirectOffsetOnAxis(ap=index, axis=0)).then_inc(xg_in, 16)

            def pool_tile(t, t1, t2, added, following):
                last = pool.value_load(tile_last[0:1, bass.ds(t, 1)], min_val=0, max_val=1)

                def next_expert(k):
                    with pool.If_ne(last.val, 0):
                        low_half(pool, following, k)

                next_expert(1)
                pool.wait_ge(xg_ps, t2)
                pool.wait_ge(src_ready, 1)
                pool.tensor_copy(gather_at[:], src_i[:, bass.ds(t2, 1)]).then_inc(gather_index, 1)
                pool.wait_ge(xn_st[XB - 1], 16 * NT // XB)
                pool.wait_ge(gather_index, t2)
                gather(gather_at[:, 0:1])
                pool.wait_ge(y_out, t1)
                pool.wait_ge(tables_ready, 1)
                pool.tensor_copy(add_at[:], dst_i[:, bass.ds(t, 1)]).then_inc(add_index, 1)
                pool.wait_ge(spare_st, 16)
                pool.wait_ge(add_index, t1)
                pool.indirect_dma_start(
                    out=acc_dram, out_offset=bass.IndirectOffsetOnAxis(ap=add_at[:, 0:1], axis=0),
                    in_=y[:], in_offset=None, compute_op=ALU.add).then_inc(y_st, 16)
                pool.wait_ge(y_st, added)

            for n in range(XB):
                pool.wait_ge(xn_st[n], 16 * NT // XB)
            for b in range(NB):
                pool.wait_ge(acc_st[b], 16 * NG)
            pool.wait_ge(src_ready, 1)
            gather(src_i[:, 0:1])
            pool.wait_ge(xg_ps, 1)
            pool.tensor_copy(gather_at[:], src_i[:, 1:2]).then_inc(gather_index, 1)
            pool.wait_ge(gather_index, 1)
            gather(gather_at[:, 0:1])
            pool.wait_ge(tables_ready, 1)
            pool_tile(0, 1, 2, 16, 1)
            with pool.Fori(1, TILES) as t:
                live = pool.value_load(tile_expert[0:1, bass.ds(t, 1)], min_val=0, max_val=E)
                with pool.If_ne(live.val, 0):
                    pool_tile(t, pool.snap(t + 1), pool.snap(t + 2), pool.snap(t * 16 + 16), live)
                    pool.nop()
            pool.sem_inc(all_added, 1)

        @block.scalar
        def _(act):
            act.dma_start(mixw[:], w_mix).then_inc(small_in, 16)
            act.dma_start(gatew[:], gate_w).then_inc(small_in, 16)
            for n in range(NS):
                act.dma_start(taps_nat[n][:], taps_dram[n].rearrange("(blk m) o k -> m blk (o k)", m=D)
                              ).then_inc(taps_in, 16)

            def copy(out, in_):
                return act.activation(out, in_, ACT.Copy)

            act.wait_ge(taps_ps, 1)
            act.wait_ge(taps_zeroed, NS)
            for n, k in enumerate(TAPS):
                for p in range(NQ):
                    at, rows_p = LAGS[n] - k - p, slice(D * p, D * p + D)
                    copy(taps[n][rows_p, :, at:at + k],
                                    taps_view(n)[rows_p, :].rearrange("r (blk k) -> r blk k", k=k)).then_inc(taps_out, 1)

            def x_turned(c):
                for b in range(NB):
                    act.wait_ge(xt_ps0, NB * c + b + 1)
                    act.activation(xs[:, 4 * c:4 * c + 4, b, PAD:], B[2 + b][:].rearrange("p (k i) -> p k i", i=P),
                                   ACT.Copy).then_inc(xs_out, 1)

            def deviation(c):
                act.wait_ge(var_in, c + 1)
                act.activation(mom[:, c % 2, 3, :], mom[:, c % 2, 3, :], ACT.Sqrt).then_inc(sd_out, 1)

            def x_high(c):
                act.wait_ge(xs_norm, c + 1)
                blocks = slice(4 * c, 4 * c + 4)
                act.activation(xs_hi[:, blocks, :, :], xs[:, blocks, :, :], ACT.Copy).then_inc(xs_hi_out, 1)

            def wc_high(i):
                cols = slice(0, head_columns(i))
                act.wait_ge(wc_ready, i + 1)
                act.activation(wc_hi[:, i % WB, cols], wc[:, i % WB, cols], ACT.Copy).then_inc(wc_hi_out, 1)

            def convolved(i):
                act.wait_ge(conv_ps, i + 1)
                if i >= 8:
                    act.wait_ge(ct_ps, 4 * (i // 4 - 1))
                act.activation(cs[:, i % 8, :, :], B[i % 2][:].rearrange("p (b i) -> p b i", i=P),
                               ACT.Copy).then_inc(conv_out, 1)

            x_turned(0)
            wc_high(0)
            x_turned(1)
            deviation(0)
            wc_high(1)
            wc_high(2)
            to_blocks(act, copy, 2)
            x_turned(2)
            act.wait_ge(pads, 1)
            x_high(0)
            deviation(1)
            to_blocks(act, copy, 3)
            x_turned(3)
            x_high(1)
            deviation(2)
            x_high(2)
            convolved(0)
            wc_high(3)
            deviation(3)
            x_high(3)
            convolved(1)
            wc_high(4)
            for i in range(2, STEPS):
                if i < NBLK:
                    convolved(i)
                n = i - 5
                if 0 <= n < NT:
                    act.wait_ge(tok_ps, n + 1)
                    act.activation(tokens(n), B[4 + n % 2][:], ACT.Copy).then_inc(tok_out, 1)
                    act.wait_ge(tok_out, n + 1)
                    act.dma_start(acc_dram[P * col(n):P * col(n) + P, :], tokens(n)).then_inc(acc_st[n % NB], 16)
                    if n == 0:
                        act.dma_start(acc_dram[TOKENS:, :], tokens(0)).then_inc(spare_st, 16)
                    act.wait_ge(var_in, NG + n + 1)
                    act.activation(rstd_t[:], rstd_t[:], ACT.Sqrt).then_inc(sd_out, 1)
                n = i - 6
                if 0 <= n < NT:
                    act.wait_ge(xn_ready, n + 1)
                    act.dma_start(xn_dram[P * col(n):P * col(n) + P, :],
                                  xnb[:, n % XB, :, :].rearrange("p q i -> p (q i)")).then_inc(xn_st[n % XB], 16)
                    act.wait_ge(xnT_ps, n + 1)
                    if n >= 2:
                        act.wait_ge(logit_ps, n - 1)
                    act.activation(xnT[:, n % 2, :, :].rearrange("p q i -> p (q i)"), B[6][:], ACT.Copy).then_inc(xnT_out, 1)
                if 5 <= i + WB < NBLK:
                    wc_high(i + WB)
            for k in range(UNITS):
                high_half(act, 0, k)

            act.wait_ge(ex_in, 1)
            act.activation(ex[:], ex[:], ACT.Exp).then_inc(ex_out, 1)

            act.wait_ge(xg_ps, 1)
            act.activation(xT_hi[:], B[6][:].rearrange("p (q i) -> p q i", i=P), ACT.Copy).then_inc(xT_hi_out, 1)

            def act_tile(t, following):
                last = act.value_load(tile_last[0:1, bass.ds(t, 1)], min_val=0, max_val=1)

                def next_expert(*ks):
                    with act.If_ne(last.val, 0):
                        for k in ks:
                            act.wait_ge(unit_done, t * UNITS + (k + 1))
                            high_half(act, following, k)

                def silu(j):
                    act.wait_ge(unit_done, t * UNITS + (2 * j + 1))
                    act.activation(h[:, j, :], B[2 * j][:], ACT.Silu).then_inc(silu_out, 1)

                def hi(j):
                    act.wait_ge(hT_ps, t * 2 + (j + 1))
                    act.activation(hT_hi[:, j, :, :], B[4 + j][:].rearrange("p (c n) -> p c n", n=P),
                                   ACT.Copy).then_inc(hT_hi_out, 1)

                silu(0)
                next_expert(0, 1)
                silu(1)
                hi(0)
                next_expert(2)
                act.wait_ge(xg_ps, t + 2)
                act.activation(xT_hi[:], B[6][:].rearrange("p (q i) -> p q i", i=P),
                               ACT.Copy).then_inc(xT_hi_out, 1)
                hi(1)
                next_expert(3, 4)
                act.wait_ge(unit_done, t * UNITS + UNITS)
                if isinstance(t, int):
                    act.wait_ge(gate_ready, 1)
                else:
                    act.wait_ge(y_st, t * 16)
                act.activation(y[:].rearrange("p (q i) -> p q i", i=P), B[7][:].rearrange("p (i q) -> p q i", q=NQ),
                               ACT.Copy, scale=slot_gate[:, bass.ds(t, 1)]).then_inc(y_out, 1)
                act.wait_ge(y_out, t + 1)
                act.activation(y_hi[:], y[:].rearrange("p (q i) -> p q i", i=P), ACT.Copy).then_inc(y_hi_out, 1)
                next_expert(5)

            act.wait_ge(tables_ready, 1)
            act_tile(0, 1)
            with act.Fori(1, TILES) as t:
                live = act.value_load(tile_expert[0:1, bass.ds(t, 1)], min_val=0, max_val=E)
                with act.If_ne(live.val, 0):
                    act_tile(t, live)
                    act.nop()

            for m in range(0, NB * NQ, 2):
                act.wait_ge(rows_ps, m + 1)
                act.activation(ot[:, m // NQ, m % NQ, :], B[m % OB][:], ACT.Copy).then_inc(ot_out[0], 1)

        @block.tensor
        def _(pe):
            pe.wait_ge(consts, 1)
            pe.wait_ge(mix4_ready, 1)
            for j in range(NS):
                pe.transpose(B[5][:, D * j:D * j + D], mix4[:, j, :, :].rearrange("d q m -> d (q m)"), ident[0:D, 0:D])
            for q in range(NQ):
                ins = pe.transpose(B[5][:, P + E * q:P + E * q + E], gatew[:, q::NQ], ident[0:E, 0:E])
            ins.then_inc(small_ps, 1)
            pe.wait_ge(copies_ready, 1)
            pe.wait_ge(taps_in, 16 * NS)
            for n in range(NS):
                ins = pe.matmul(taps_view(n), copies[:].rearrange("d q m -> d (q m)"),
                                taps_nat[n][:].rearrange("m blk k -> m (blk k)"), start=True, stop=True)
            ins.then_inc(taps_ps, 1)

            def moments(c):
                for k in range(2):
                    pe.wait_ge(mom_ready, 2 * c + k + 1)
                    pe.matmul(B[6 + k][:, NBLK * c:NBLK * c + NBLK], same[:], mom[:, c % 2, (0, 4)[k], :],
                              start=True, stop=True).then_inc(mom_ps, 1)

            pe.wait_ge(pool_step, 6)

            def turn_x(c):
                for b in range(NB):
                    pe.wait_ge(x_blocks[c], b + 1)
                    if c >= 1:
                        pe.wait_ge(xs_out, NB * (c - 1) + b + 1)
                    for k in range(4):
                        ins = pe.transpose(B[2 + b][:, P * k:P * k + P],
                                           X[:, b, 4 * c + k, :, :].rearrange("p q d -> p (q d)"), ident[:])
                    ins.then_inc(xt_ps0, 1)

            def conv(i):
                parts = [(blk, d) for n, blk, _ in head_parts(i) for d in range(LAGS[n] // NQ)]
                quarters = max(p[0] for p in parts) // 4 + 1
                pe.wait_ge(xs_lo_out, min(quarters, NG - 1))
                if quarters == NG:
                    pe.wait_ge(last_lo_out, 1)
                pe.wait_ge(wc_lo_out, i + 1)
                if i >= 2:
                    pe.wait_ge(conv_out, i - 1)
                out = B[i % 2][:].rearrange("p (b i) -> p b i", i=P)
                for a, (blk, d) in enumerate(parts):
                    cols, at = slice(P * a, P * a + P), slice(PAD - d, PAD - d + P)
                    pe.matmul(out, wc_hi[:, i % WB, cols], xs_hi[:, blk, :, at], start=(a == 0), stop=False)
                    pe.matmul(out, wc_hi[:, i % WB, cols], xs_lo[:, blk, :, at], start=False, stop=False)
                    ins = pe.matmul(out, wc_lo[:, i % WB, cols], xs_hi[:, blk, :, at],
                                    start=False, stop=(a == len(parts) - 1))
                ins.then_inc(conv_ps, 1)

            turn_x(0)
            turn_x(1)
            moments(0)
            turn_x(2)
            moments(1)
            turn_x(3)
            conv(0)
            moments(2)
            conv(1)
            moments(3)
            def count(g, tiles):
                pe.wait_ge(lg_out, tiles)
                pe.wait_ge(consts, CONSTS)
                pe.wait_ge(mask_ready, g + 1)
                first, stop = BATCHES[g]
                for at, weights in ((P, below), (2 * P, ones)):
                    for j in range(2):
                        ins = pe.matmul(B[7][:, at + E * first:at + E * stop], weights[:],
                                        masks[:, j, first:stop, :].rearrange("p t e -> p (t e)"),
                                        start=(j == 0), stop=(j == 1))
                ins.then_inc(count_ps, 1)

            for i in range(2, STEPS):
                if i < NBLK:
                    conv(i)
                g = counted_at(i)
                if g is not None:
                    count(g, i - 7)
                n = i - 4
                if 0 <= n < NT:
                    g, b = gb(n)
                    pe.wait_ge(conv_out, 4 * g + 4)
                    if n >= 2:
                        pe.wait_ge(resid, n - 1)
                    for k in range(4):
                        ins = pe.transpose(B[2 + n % 2][:, P * k:P * k + P], cs[:, (4 * g + k) % 8, b, :], ident[:])
                    ins.then_inc(ct_ps, 1)
                n = i - 5
                if 0 <= n < NT:
                    g, b = gb(n)
                    pe.wait_ge(resid, n + 1)
                    if n >= 2:
                        pe.wait_ge(tok_out, n - 1)
                    for q in range(NQ):
                        ins = pe.transpose(B[4 + n % 2][:, P * q:P * q + P], xc[:, n % 2, q, :], ident[:])
                    ins.then_inc(tok_ps, 1)
                n = i - 6
                if 0 <= n < NT:
                    pe.wait_ge(xn_ready, n + 1)
                    if n >= 1:
                        pe.wait_ge(xnT_out, n)
                    for q in range(NQ):
                        ins = pe.transpose(B[6][:, P * q:P * q + P], xnb[:, n % XB, q, :], ident[:])
                    ins.then_inc(xnT_ps, 1)
                n = i - 7
                if 0 <= n < NT:
                    pe.wait_ge(xnT_out, n + 1)
                    if n >= 1:
                        pe.wait_ge(lg_out, n)
                    if counted_at(i) is not None:
                        pe.wait_ge(count_out, counted_at(i) + 1)
                    for q in range(NQ):
                        ins = pe.matmul(B[7][:, E * n:E * n + E], xnT[:, n % 2, q, :], gateT[:, q, :],
                                        start=(q == 0), stop=(q == NQ - 1))
                    ins.then_inc(logit_ps, 1)
            count(len(BATCHES) - 1, NT)

            for a in range(2 * NT):
                if a % 8 == 0:
                    pe.wait_ge(rows_hot, a // 8 + 1)
                ins = pe.matmul(B[2][:, 0:SLOT_TILES], row_hot[:, a, :], hot_token[:, a, :],
                                start=(a == 0), stop=(a == 2 * NT - 1))
            ins.then_inc(slot_ps, 1)

            def slot_weights():
                pe.wait_ge(gates_hot, 1)
                for a in range(2 * NT):
                    ins = pe.matmul(B[5][:, 0:2 * SLOT_TILES], row_hot[:, a, :],
                                    hot_gate[:, a, :, :].rearrange("p v t -> p (v t)"),
                                    start=(a == 0), stop=(a == 2 * NT - 1))
                ins.then_inc(gate_ps, 1)

            def turn_tokens(n):
                pe.wait_ge(xg_in, n * 16)
                for q in range(NQ):
                    ins = pe.transpose(B[6][:, P * q:P * q + P], xg[:, q, :], ident[:])
                ins.then_inc(xg_ps, 1)

            def product(bank, stat_hi, stat_lo, k, c, start, stop):
                hi, lo = w_hi[:, k, c, :], w_lo[:, k, c, :]
                pe.matmul(B[bank][:], stat_hi, hi, start=start, stop=False)
                pe.matmul(B[bank][:], stat_hi, lo, start=False, stop=False)
                return pe.matmul(B[bank][:], stat_lo, hi, start=False, stop=stop)

            def pe_tile(t, split):
                def up(k):
                    pe.wait_ge(lo_ready[k], split)
                    for c in range(4):
                        ins = product(k, xT_hi[:, c, :], xT_lo[:, c, :], k, c, c == 0, c == 3)
                    ins.then_inc(unit_done, 1)

                def turn_h(j):
                    pe.wait_ge(h_out, t * 2 + (j + 1))
                    for c in range(4):
                        ins = pe.transpose(B[4 + j][:, P * c:P * c + P], h[:, j, P * c:P * c + P], ident[:])
                    ins.then_inc(hT_ps, 1)

                def down(j, chunks):
                    for c in chunks:
                        ins = product(7, hT_hi[:, j, c, :], hT_lo[:, j, c, :], 4 + j, c,
                                      j == 0 and c == 0, j == 1 and c == 3)
                    return ins

                pe.wait_ge(xT_lo_out, t + 1)
                up(0)
                up(1)
                if isinstance(t, int):
                    slot_weights()
                up(2)
                turn_h(0)
                up(3)
                turn_tokens(t + 2)
                pe.wait_ge(lo_ready[4], split)
                pe.wait_ge(hT_lo_out, t * 2 + 1)
                if not isinstance(t, int):
                    pe.wait_ge(y_out, t)
                down(0, (0,))
                turn_h(1)
                down(0, (1, 2, 3)).then_inc(unit_done, 1)
                pe.wait_ge(lo_ready[5], split)
                pe.wait_ge(hT_lo_out, t * 2 + 2)
                down(1, range(4)).then_inc(unit_done, 1)

            turn_tokens(1)
            pe_tile(0, 1)
            pe.wait_ge(tables_ready, 1)
            with pe.Fori(1, TILES) as t:
                split = pe.value_load(tile_expert[0:1, bass.ds(t, 1)], min_val=0, max_val=E)
                with pe.If_ne(split.val, 0):
                    pe_tile(t, split)

            def turn_rows(m):
                b, q = divmod(m, NQ)
                pe.wait_ge(rows_in[b], 16)
                if m >= OB:
                    pe.wait_ge(ot_out[m % 2], (m - OB) // 2 + 1)
                for g in range(NG):
                    pe.matmul(B[m % OB][:, P * g:P * g + P], rows[:, b, g, P * q:P * q + P], ident[:],
                              is_transpose=True, start=(g == 0), stop=False)

            def add_last(m):
                b, q = divmod(m, NQ)
                pe.matmul(B[m % OB][:], y_hi[:, q, :], last_hot[:, C * b:C * b + C], start=False, stop=False)
                ins = pe.matmul(B[m % OB][:], y_lo[:, q, :], last_hot[:, C * b:C * b + C], start=False, stop=True)
                ins.then_inc(rows_ps, 1)

            for m in range(4):
                turn_rows(m)
            pe.wait_ge(y_lo_out, 1)
            for m in range(NB * NQ):
                if m % NQ == 0:
                    pe.wait_ge(last_hot_ready, m // NQ + 1)
                add_last(m)
                if m + 4 < NB * NQ:
                    turn_rows(m + 4)

        @block.vector
        def _(dve):
            steps = [0]

            def then_next(ins):
                steps[0] += 1
                ins.then_inc(dve_step, 1)
                dve.wait_ge(dve_step, steps[0])

            dve.wait_ge(consts, 1)
            dve.tensor_copy(copies[:], ident[0:D, 0:D].unsqueeze(1).broadcast_to([D, NQ, D])).then_inc(copies_ready, 1)
            dve.wait_ge(small_in, 32)
            dve.tensor_copy(mix4[:], mixw[:].rearrange("d (j m) -> d j m", j=NS).unsqueeze(2)
                            .broadcast_to([D, NS, NQ, D])).then_inc(mix4_ready, 1)
            dve.wait_ge(small_ps, 1)
            dve.tensor_copy(mixT[:], B[5][:, 0:NS * D].rearrange("p (j d) -> p j d", d=D)).then_inc(small_out, 1)
            dve.tensor_copy(gateT[:], B[5][:, P:P + NQ * E].rearrange("p (q e) -> p q e", e=E)).then_inc(small_out, 1)

            def moment(c, k):
                return mom[:, c % 2, k, :]

            def row_moments(c):
                for b in range(NB):
                    dve.wait_ge(xs_out, NB * c + b + 1)
                    for k in range(4):
                        ins = dve.bn_stats(bn6[:, NB * k + b, :], xs[:, 4 * c + k, b, PAD:])
                then_next(ins)
                mean, dm, var = (moment(c, k) for k in range(3))
                dve.tensor_tensor(mean, bn6[:, :, 1], bn6[:, :, 4], ALU.add)
                then_next(dve.tensor_tensor(dm, bn6[:, :, 1], bn6[:, :, 4], ALU.subtract))
                dve.tensor_scalar(mean, mean, 0.5, None, ALU.mult).then_inc(mom_ready, 1)
                dve.tensor_tensor(var, bn6[:, :, 2], bn6[:, :, 5], ALU.add)
                then_next(dve.tensor_tensor(dm, dm, dm, ALU.mult))
                then_next(dve.scalar_tensor_tensor(out=var, in0=dm, scalar=P / 4.0, in1=var, op0=ALU.mult, op1=ALU.add))

            def second_moment(c):
                mean, var, dev, mean_all = (moment(c, k) for k in (0, 2, 3, 5))
                dve.wait_ge(mom_ps, 2 * c + 1)
                then_next(dve.tensor_copy(mean_all, B[6][:, NBLK * c:NBLK * c + NBLK]))
                then_next(dve.tensor_tensor(dev, mean, mean_all, ALU.subtract))
                then_next(dve.tensor_tensor(dev, dev, dev, ALU.mult))
                dve.scalar_tensor_tensor(out=moment(c, 4), in0=var, scalar=1.0 / P, in1=dev,
                                         op0=ALU.mult, op1=ALU.add).then_inc(mom_ready, 1)

            def variance(c):
                dve.wait_ge(mom_ps, 2 * c + 2)
                dve.tensor_scalar(moment(c, 3), B[7][:, NBLK * c:NBLK * c + NBLK], EPS_C, None,
                                  ALU.add).then_inc(var_in, 1)

            def normalise(c):
                dev, mean_all = moment(c, 3), moment(c, 5)
                dve.wait_ge(sd_out, c + 1)
                then_next(dve.reciprocal(dev, dev))
                for k in range(4):
                    for b in range(NB):
                        m, v = NB * k + b, xs[:, 4 * c + k, b, PAD:]
                        ins = dve.tensor_scalar(v, v, mean_all[:, m:m + 1], dev[:, m:m + 1], ALU.subtract, ALU.mult)
                ins.then_inc(xs_norm, 1)

            for c in range(2):
                to_blocks(dve, dve.tensor_copy, c)
            row_moments(0)
            for c in range(NG):
                second_moment(c)
                variance(c)
                if c + 1 < NG:
                    row_moments(c + 1)
                normalise(c)
            x_low(dve, NG - 1)

            def pick_first(values, biggest, mask):
                shape = [P, values.shape[1], E]
                chosen, number = sel[:, 0:shape[1], :], pick[:, 0:shape[1]]
                ranks = rank8[:].unsqueeze(1).broadcast_to(shape)
                then_next(dve.tensor_tensor(chosen, values, biggest.unsqueeze(2).broadcast_to(shape), ALU.is_equal))
                then_next(dve.tensor_tensor(chosen, chosen, ranks, ALU.mult))
                then_next(dve.tensor_reduce(number, chosen, AX_X, ALU.max))
                return dve.tensor_tensor(mask, ranks, number.unsqueeze(2).broadcast_to(shape), ALU.is_equal)

            def mask_batch(g):
                tiles = slice(*BATCHES[g])
                n = tiles.stop - tiles.start
                lg, top = logits[:, tiles, :], top1[:, tiles]
                dve.wait_ge(lg_out, tiles.stop)
                then_next(dve.tensor_reduce(top, lg, AX_X, ALU.max))
                then_next(pick_first(lg, top, masks[:, 0, tiles, :]))
                then_next(dve.scalar_tensor_tensor(out=rest[:, 0:n, :], in0=masks[:, 0, tiles, :], scalar=-3.0e38, in1=lg,
                                                   op0=ALU.mult, op1=ALU.add))
                then_next(dve.tensor_reduce(top2[:, 0:n], rest[:, 0:n, :], AX_X, ALU.max))
                pick_first(rest[:, 0:n, :], top2[:, 0:n], masks[:, 1, tiles, :]).then_inc(mask_ready, 1)

            def count_batch(g):
                dve.wait_ge(count_ps, g + 1)
                tiles = slice(*BATCHES[g])
                dve.tensor_copy(counts[:, :, tiles, :], B[7][:, P:3 * P].rearrange(
                    "p (v t e) -> p v t e", v=2, e=E)[:, :, tiles, :]).then_inc(count_out, 1)
                dve.wait_ge(count_out, g + 1)
                for n in range(*BATCHES[g]):
                    then_next(dve.tensor_tensor(running[:, n + 1, :], running[:, n, :], counts[:, 1, n, :], ALU.add))

            dve.memset(running[:, 0, :], 0.0)
            dve.wait_ge(consts, CONSTS)
            then_next(dve.tensor_tensor(earlier[:], rank8[:].unsqueeze(1).broadcast_to([P, E, E]),
                                        rank8[:].unsqueeze(2).broadcast_to([P, E, E]), ALU.is_gt))
            for i in range(EARLY - WB, STEPS):
                if counted_at(i) is not None:
                    count_batch(counted_at(i))
                n = i - 4
                if 0 <= n < NT:
                    g, b = gb(n)
                    dve.wait_ge(ct_ps, n + 1)
                    if n >= 2:
                        dve.wait_ge(tok_ps, n - 1)
                    dve.tensor_tensor(xc[:, n % 2, :, :].rearrange("p q (k d) -> p k q d", d=D),
                                      B[2 + n % 2][:].rearrange("p (k q d) -> p k q d", q=NQ, d=D),
                                      X[:, b, 4 * g:4 * g + 4, :, :], ALU.add).then_inc(resid, 1)
                n = i - 5
                if 0 <= n < NT:
                    dve.wait_ge(tok_out, n + 1)
                    then_next(dve.bn_stats(st6[:], tokens(n)))
                    then_next(dve.bn_aggr(mv[:], st6[:]))
                    dve.tensor_scalar(rstd_t[:], mv[:, 1:2], EPS_T, None, ALU.add).then_inc(var_in, 1)
                    dve.wait_ge(sd_out, NG + n + 1)
                    then_next(dve.reciprocal(rstd_t[:], rstd_t[:]))
                    if n >= XB:
                        dve.wait_ge(xn_st[n % XB], 16 * (n // XB))
                        dve.wait_ge(xnT_ps, n + 1 - XB)
                    dve.tensor_scalar(xnb[:, n % XB, :, :].rearrange("p q i -> p (q i)"), tokens(n), mv[:, 0:1], rstd_t[:],
                                      ALU.subtract, ALU.mult).then_inc(xn_ready, 1)
                n = i - 7
                if 0 <= n < NT:
                    dve.wait_ge(logit_ps, n + 1)
                    dve.tensor_copy(logits[:, n, :], B[7][:, E * n:E * n + E]).then_inc(lg_out, 1)
                if EARLY <= i + WB < NBLK:
                    wc_low(dve, i + WB)
                for g, (_, stop) in enumerate(BATCHES):
                    if n + 1 == stop:
                        mask_batch(g)

            count_batch(len(BATCHES) - 1)
            for b in range(2):
                dve.wait_ge(acc_st[b], 16 * NG)
            cnt = running[:, NT, :]
            then_next(dve.tensor_tensor(over[:], cnt.unsqueeze(2).broadcast_to([P, E, 16]),
                                        thresholds[:].unsqueeze(1).broadcast_to([P, E, 16]), ALU.is_gt))
            dve.tensor_tensor(base[:], counts[:, 0, :, :], running[:, 0:NT, :], ALU.add)
            then_next(dve.tensor_reduce(ntile[:], over[:], AX_X, ALU.add))
            then_next(dve.tensor_scalar(ntile[:], ntile[:], 1.0, None, ALU.max))
            then_next(dve.tensor_tensor(upto[:], earlier[:], ntile[:].unsqueeze(1).broadcast_to([P, E, E]), ALU.mult))
            then_next(dve.tensor_reduce(start_t[:], upto[:], AX_X, ALU.add))
            then_next(dve.scalar_tensor_tensor(out=base[:], in0=start_t[:].unsqueeze(1).broadcast_to([P, NT, E]),
                                               scalar=float(P), in1=base[:], op0=ALU.mult, op1=ALU.add))
            then_next(dve.tensor_tensor(picked[:], masks[:], base[:].unsqueeze(1).broadcast_to([P, 2, NT, E]), ALU.mult))
            slot = small[:, 5, :]
            then_next(dve.tensor_reduce(slot, picked[:].rearrange("p j t e -> p (j t) e"), AX_X, ALU.add))
            then_next(dve.tensor_copy(sl_i[:, 2, :], slot))
            dve.tensor_scalar(sl_i[:, 0, :], sl_i[:, 2, :], 7, None, ALU.arith_shift_right)
            then_next(dve.tensor_scalar(sl_i[:, 1, :], sl_i[:, 2, :], P - 1, None, ALU.bitwise_and))
            then_next(dve.tensor_copy(sl_f[:], sl_i[:, 0:2, :]))

            def hot_rows(k):
                pairs = slice(8 * k, 8 * k + 8)
                dve.tensor_tensor(row_hot[:, pairs, :], iota[:].unsqueeze(1).broadcast_to([P, 8, P]),
                                  sl_f[:, 1, pairs].unsqueeze(2).broadcast_to([P, 8, P]), ALU.is_equal).then_inc(rows_hot, 1)

            for b in range(2, NB):
                dve.wait_ge(acc_st[b], 16 * NG)
            for j in range(2):
                pairs = slice(NT * j, NT * j + NT)
                shape = [P, NT, SLOT_TILES]
                then_next(dve.tensor_tensor(hot[:, pairs, :], iota[:, 0:SLOT_TILES].unsqueeze(1).broadcast_to(shape),
                                            sl_f[:, 0, pairs].unsqueeze(2).broadcast_to(shape), ALU.is_equal))
                dve.tensor_tensor(hot_token[:, pairs, :], hot[:, pairs, :],
                                  tokid[:].unsqueeze(2).broadcast_to(shape), ALU.mult)
                for k in range(2):
                    hot_rows(2 * j + k)

            then_next(dve.tensor_tensor(end[:], start_t[:], ntile[:], ALU.add))
            then_next(dve.tensor_tensor(passed[:], iota[0:1, 0:SLOT_TILES].unsqueeze(2).broadcast_to([1, SLOT_TILES, E]),
                                        end[0:1, :].unsqueeze(1).broadcast_to([1, SLOT_TILES, E]), ALU.is_ge))
            expert, live, following = (te[:, k, :] for k in range(3))
            then_next(dve.tensor_reduce(expert, passed[:], AX_X, ALU.add))
            dve.wait_ge(slot_ps, 1)
            dve.tensor_scalar(src_i[:], B[2][:, 0:SLOT_TILES], 1.0, 0.0, ALU.subtract, ALU.max).then_inc(src_ready, 1)
            dve.tensor_copy(number[:], B[2][:, 0:SLOT_TILES])
            dve.tensor_scalar(live, expert, float(E), None, ALU.is_lt)
            then_next(dve.tensor_scalar(following, expert, 1.0, None, ALU.add))
            dve.tensor_tensor(tile_expert[:], following[:, 0:TILES], live[:, 0:TILES], ALU.mult)
            dve.tensor_scalar(expert, expert, float(E - 1), None, ALU.min)
            then_next(dve.tensor_scalar(last_token[:, 0:1], end[:, E - 1:E], 1.0, None, ALU.subtract))
            dve.tensor_copy(tiles_before[:], last_token[0:1, 0:1])
            dve.tensor_tensor(tile_last[:], expert[:, 1:TILES + 1], expert[:, 0:TILES], ALU.subtract)
            then_next(dve.tensor_scalar(final[:], iota[:, 0:SLOT_TILES], last_token[:, 0:1], None, ALU.is_equal))
            dve.tensor_scalar(empty[:], number[:], 0.0, None, ALU.is_equal)
            then_next(dve.tensor_tensor(last_number[:], final[:], number[:], ALU.mult))
            dve.tensor_tensor(empty[:], empty[:], final[:], ALU.max)
            then_next(dve.tensor_reduce(last_token[:, 1:2], last_number[:], AX_X, ALU.add))
            dve.tensor_tensor(number[:], number[:], last_number[:], ALU.subtract)
            then_next(dve.tensor_tensor(empty[:], empty[:], spare[:], ALU.mult))
            then_next(dve.tensor_scalar(last_token[:, 1:2], last_token[:, 1:2], 1.0, None, ALU.subtract))
            dve.tensor_scalar(last_at[:], thresholds[:, 0:NT], last_token[:, 1:2], -1.0, ALU.subtract, ALU.mult)
            dve.scalar_tensor_tensor(out=dst_i[:], in0=number[:], scalar=-1.0, in1=empty[:],
                                     op0=ALU.add, op1=ALU.add).then_inc(tables_ready, 1)

            def xT_rest(n):
                dve.wait_ge(xT_hi_out, n)
                dve.tensor_tensor(xT_lo[:], B[6][:].rearrange("p (q i) -> p q i", i=P), xT_hi[:],
                                  ALU.subtract).then_inc(xT_lo_out, 1)

            dve.tensor_tensor(ex[:], logits[:],
                              top1[:].unsqueeze(2).broadcast_to([P, NT, E]), ALU.subtract).then_inc(ex_in, 1)
            total, rsum, psum2 = (small[:, k, 0:NT] for k in range(3))
            pk, gate = (small[:, k, :] for k in (3, 4))
            dve.wait_ge(ex_out, 1)
            then_next(dve.tensor_reduce(total, ex[:], AX_X, ALU.add))
            then_next(dve.reciprocal(rsum, total))
            then_next(dve.tensor_tensor(ex[:], ex[:], rsum.unsqueeze(2).broadcast_to([P, NT, E]), ALU.mult))
            then_next(dve.tensor_tensor(picked[:], masks[:], ex[:].unsqueeze(1).broadcast_to([P, 2, NT, E]), ALU.mult))
            then_next(dve.tensor_reduce(pk, picked[:].rearrange("p j t e -> p (j t) e"), AX_X, ALU.add))
            then_next(dve.tensor_tensor(psum2, pk[:, 0:NT], pk[:, NT:], ALU.add))
            then_next(dve.reciprocal(psum2, psum2))
            then_next(dve.tensor_tensor(gate.rearrange("p (j t) -> p j t", j=2), pk.rearrange("p (j t) -> p j t", j=2),
                                        psum2.unsqueeze(1).broadcast_to([P, 2, NT]), ALU.mult))
            then_next(dve.tensor_copy(gate_hi[:], gate))
            then_next(dve.tensor_tensor(gate_lo[:], gate, gate_hi[:], ALU.subtract))
            xT_rest(1)
            for v, half in enumerate((gate_hi, gate_lo)):
                ins = dve.tensor_tensor(hot_gate[:, :, v, :], hot[:],
                                        half[:].unsqueeze(2).broadcast_to([P, 2 * NT, SLOT_TILES]), ALU.mult)
            ins.then_inc(gates_hot, 1)

            def dve_tile(t, following):
                last = dve.value_load(tile_last[0:1, bass.ds(t, 1)], min_val=0, max_val=1)

                def next_expert(*ks):
                    with dve.If_ne(last.val, 0):
                        for k in ks:
                            low_half(dve, following, k)

                def gate_up(j):
                    dve.wait_ge(silu_out, t * 2 + (j + 1))
                    dve.wait_ge(unit_done, t * UNITS + (2 * j + 2))
                    dve.tensor_tensor(h[:, j, :], B[2 * j + 1][:], h[:, j, :], ALU.mult).then_inc(h_out, 1)

                def rest_of_hT(j):
                    dve.wait_ge(hT_hi_out, t * 2 + (j + 1))
                    dve.tensor_tensor(hT_lo[:, j, :, :], B[4 + j][:].rearrange("p (c n) -> p c n", n=P),
                                      hT_hi[:, j, :, :], ALU.subtract).then_inc(hT_lo_out, 1)

                gate_up(0)
                next_expert(0)
                rest_of_hT(0)
                gate_up(1)
                xT_rest(t + 2)
                rest_of_hT(1)
                next_expert(2, 3, 4, 5)

            for k in range(POOL_UNITS, UNITS):
                low_half(dve, 0, k)
            dve.wait_ge(gate_ps, 1)
            then_next(dve.tensor_copy(slot_gate[:], B[5][:, SLOT_TILES:2 * SLOT_TILES]))
            dve.tensor_tensor(slot_gate[:], slot_gate[:], B[5][:, 0:SLOT_TILES], ALU.add).then_inc(gate_ready, 1)
            dve_tile(0, 1)
            with dve.Fori(1, TILES) as t:
                live = dve.value_load(tile_expert[0:1, bass.ds(t, 1)], min_val=0, max_val=E)
                with dve.If_ne(live.val, 0):
                    dve_tile(t, live)
                    dve.nop()

            before = dve.value_load(tiles_before[0:1, 0:1], min_val=E - 1, max_val=TILES - 1)
            dve.wait_ge(y_hi_out, before + 1)
            dve.tensor_tensor(y_lo[:], y[:].rearrange("p (q i) -> p q i", i=P), y_hi[:], ALU.subtract).then_inc(y_lo_out, 1)
            for k in range(UNITS):
                dve.wait_ge(lo_ready[k], E)
            for k in range(NT):
                ins = dve.tensor_scalar(last_hot[:, P * k:P * k + P], iota[:], last_at[:, k:k + 1], None, ALU.is_equal)
                if k % NG == NG - 1:
                    ins.then_inc(last_hot_ready, 1)
            for m in range(1, NB * NQ, 2):
                dve.wait_ge(rows_ps, m + 1)
                dve.tensor_copy(ot[:, m // NQ, m % NQ, :], B[m % OB][:]).then_inc(ot_out[1], 1)


_INS = ["x", "L0_conv_w3", "L0_conv_w7", "L0_conv_w15", "L0_conv_w_mix", "L0_ffn_gate_w",
        "L0_ffn_w1", "L0_ffn_w2", "L0_ffn_w3"]


def kernel(**inputs):
    import numpy as _np
    import concourse.bacc as _bacc
    from concourse import mybir as _mybir
    from concourse.bass_utils import run_bass_kernel_spmd as _run

    nc = _bacc.Bacc("TRN2", target_bir_lowering=False, num_devices=1)
    arrays, args = {}, []
    for name in _INS:
        a = _np.ascontiguousarray(inputs[name])
        arrays[f"in_{name}"] = a
        args.append(nc.dram_tensor(f"in_{name}", a.shape, _mybir.dt.from_np(a.dtype), kind="ExternalInput").ap())
    args.append(nc.dram_tensor("out_x", inputs["x"].shape, F32, kind="ExternalOutput").ap())
    metaformer(nc, *args)
    r = _run(nc, [arrays], core_ids=[0])
    return r.results[0]["out_x"]
```
